# Optimizing a Trainium2 kernel written in Bass

```python
import numpy as np
import jax
import jax.numpy as jnp

def _softmax(x, axis=-1):
    return jax.nn.softmax(x, axis=axis)

def _gelu(x):
    return jax.nn.gelu(x, approximate=True)

def _silu(x):
    return jax.nn.silu(x)

def _sigmoid(x):
    return jax.nn.sigmoid(x)

def _layernorm(x, axis=-1, eps=1e-05):
    m = jnp.mean(x, axis=axis, keepdims=True)
    v = jnp.var(x, axis=axis, keepdims=True)
    return (x - m) / jnp.sqrt(v + eps)

def _scatter_add(tgt, idx, src, axis=0):
    return tgt.at[idx].add(src)

def _segment_sum(src, seg, n):
    return jax.ops.segment_sum(src, seg, n)
kernel_name = 'mk_cond_resid_d2_seqx_r4_eb20ec'

def setup_inputs(seed: int=0):
    np.random.seed(seed)
    _w = jnp.asarray

    def _rec_inputs():
        import jax
        import jax.numpy as jnp
        _rk = jax.random.key(seed)
        x = -0.0001538 + 1 * jax.random.normal(jax.random.fold_in(_rk, 1), (2, 1024, 256), jnp.float32)
        _lenS = 1024 - jax.random.randint(jax.random.fold_in(_rk, 7), (2,), 0, max(1, 1024 // 4) + 1, jnp.int32)
        _lenS2 = 1024 - jax.random.randint(jax.random.fold_in(_rk, 8), (2,), 0, max(1, 1024 // 4) + 1, jnp.int32)
        cond_1024 = 0.00782532 + 1.00527 * jax.random.normal(jax.random.fold_in(_rk, 11), (2, 256), jnp.float32)
        return (x, cond_1024)
    x, cond_1024 = _rec_inputs()

    def _L0_cond_setup():
        import jax, jax.numpy as jnp
        import numpy as np
        NUM_EXPERTS = 4
        TOP_K = 2
        key = jax.random.key(seed)
        ks = jax.random.split(key, 16)
        B, L, D, E, H = (8, 192, 256, NUM_EXPERTS, 1024)
        s = 0.02
        return {'context_c': jax.random.normal(ks[0], (B, L, D), jnp.float32), 'time_cond': jax.random.normal(ks[1], (B, D), jnp.float32), 'gate_w': jax.random.normal(ks[2], (3 * D, E), jnp.float32) * s, 'gate_b': jnp.zeros((E,), jnp.float32), 'time_w': jax.random.normal(ks[3], (D, 2 * E), jnp.float32) * s, 'time_b': jnp.zeros((2 * E,), jnp.float32), 'ew1': jax.random.normal(ks[4], (E, D, H), jnp.float32) * s, 'eb1': jnp.zeros((E, H), jnp.float32), 'ew2': jax.random.normal(ks[5], (E, H, D), jnp.float32) * s, 'eb2': jnp.zeros((E, D), jnp.float32), 'sw1': jax.random.normal(ks[6], (D, H), jnp.float32) * s, 'sb1': jnp.zeros((H,), jnp.float32), 'sw2': jax.random.normal(ks[7], (H, D), jnp.float32) * s, 'sb2': jnp.zeros((D,), jnp.float32)}
    _L0_cond_all = _L0_cond_setup()
    _L0_cond_in = {k: v for k, v in _L0_cond_all.items() if k in ('gate_w', 'gate_b', 'time_w', 'time_b', 'ew1', 'eb1', 'ew2', 'eb2', 'sw1', 'sb1', 'sw2', 'sb2')}
    del _L0_cond_all

    def _L1_cond_setup():
        import jax, jax.numpy as jnp
        import numpy as np
        B, T, D_IN, V_IN, E = (64, 128, 256, 256, 256)
        key = jax.random.key(seed)
        ks = jax.random.split(key, 16)
        s = 0.01
        return {'video': jax.random.normal(ks[0], (B, V_IN), jnp.float32), 'seq': jax.random.normal(ks[1], (B, T, D_IN), jnp.float32), 'W_z': jax.random.normal(ks[2], (D_IN, E), jnp.float32) * s, 'U_z': jax.random.normal(ks[3], (E, E), jnp.float32) * s, 'C_z': jax.random.normal(ks[4], (V_IN, E), jnp.float32) * s, 'b_z': jnp.zeros((E,), jnp.float32), 'W_r': jax.random.normal(ks[5], (D_IN, E), jnp.float32) * s, 'U_r': jax.random.normal(ks[6], (E, E), jnp.float32) * s, 'C_r': jax.random.normal(ks[7], (V_IN, E), jnp.float32) * s, 'b_r': jnp.zeros((E,), jnp.float32), 'W': jax.random.normal(ks[8], (D_IN, E), jnp.float32) * s, 'U': jax.random.normal(ks[9], (E, E), jnp.float32) * s, 'C': jax.random.normal(ks[10], (V_IN, E), jnp.float32) * s, 'b': jnp.zeros((E,), jnp.float32)}
    _L1_cond_all = _L1_cond_setup()
    _L1_cond_in = {k: v for k, v in _L1_cond_all.items() if k in ('W_z', 'U_z', 'C_z', 'b_z', 'W_r', 'U_r', 'C_r', 'b_r', 'W', 'U', 'C', 'b')}
    del _L1_cond_all
    return {'x': x, 'cond_1024': cond_1024, 'L0_cond_gate_w': _L0_cond_in['gate_w'], 'L0_cond_gate_b': _L0_cond_in['gate_b'], 'L0_cond_time_w': _L0_cond_in['time_w'], 'L0_cond_time_b': _L0_cond_in['time_b'], 'L0_cond_ew1': _L0_cond_in['ew1'], 'L0_cond_eb1': _L0_cond_in['eb1'], 'L0_cond_ew2': _L0_cond_in['ew2'], 'L0_cond_eb2': _L0_cond_in['eb2'], 'L0_cond_sw1': _L0_cond_in['sw1'], 'L0_cond_sb1': _L0_cond_in['sb1'], 'L0_cond_sw2': _L0_cond_in['sw2'], 'L0_cond_sb2': _L0_cond_in['sb2'], 'L1_cond_W_z': _L1_cond_in['W_z'], 'L1_cond_U_z': _L1_cond_in['U_z'], 'L1_cond_C_z': _L1_cond_in['C_z'], 'L1_cond_b_z': _L1_cond_in['b_z'], 'L1_cond_W_r': _L1_cond_in['W_r'], 'L1_cond_U_r': _L1_cond_in['U_r'], 'L1_cond_C_r': _L1_cond_in['C_r'], 'L1_cond_b_r': _L1_cond_in['b_r'], 'L1_cond_W': _L1_cond_in['W'], 'L1_cond_U': _L1_cond_in['U'], 'L1_cond_C': _L1_cond_in['C'], 'L1_cond_b': _L1_cond_in['b']}

def reference(x, cond_1024, L0_cond_gate_w, L0_cond_gate_b, L0_cond_time_w, L0_cond_time_b, L0_cond_ew1, L0_cond_eb1, L0_cond_ew2, L0_cond_eb2, L0_cond_sw1, L0_cond_sb1, L0_cond_sw2, L0_cond_sb2, L1_cond_W_z, L1_cond_U_z, L1_cond_C_z, L1_cond_b_z, L1_cond_W_r, L1_cond_U_r, L1_cond_C_r, L1_cond_b_r, L1_cond_W, L1_cond_U, L1_cond_C, L1_cond_b):
    import jax
    import jax.numpy as jnp

    def _L0_cond_ref(context_c, time_cond, gate_w, gate_b, time_w, time_b, ew1, eb1, ew2, eb2, sw1, sb1, sw2, sb2):
        import jax, jax.numpy as jnp
        import numpy as np
        NUM_EXPERTS = 4
        TOP_K = 2
        B, L, D = context_c.shape
        E, K = (NUM_EXPERTS, TOP_K)
        L_head = L_wrist = L // 3
        head = context_c[:, :L_head]
        wrist = context_c[:, L_head:L_head + L_wrist]
        proprio = context_c[:, L_head + L_wrist:]
        full_agg = context_c.mean(axis=1)
        hp_agg = jnp.concatenate([head, proprio], axis=1).mean(axis=1)
        wp_agg = jnp.concatenate([wrist, proprio], axis=1).mean(axis=1)
        gate_in = jnp.concatenate([full_agg, hp_agg, wp_agg], axis=-1)
        gate_logits = gate_in @ gate_w + gate_b
        mod = jax.nn.silu(time_cond) @ time_w + time_b
        scale, shift = jnp.split(mod, 2, axis=-1)
        gate_logits = gate_logits * (1.0 + scale) + shift
        gate_scores = jax.nn.softmax(gate_logits, axis=-1)
        topk_w, topk_i = jax.lax.top_k(gate_scores, K)
        topk_w = topk_w / (topk_w.sum(axis=-1, keepdims=True) + 1e-08)
        onehot = (topk_i[..., None] == jnp.arange(E)[None, None, :]).astype(context_c.dtype)
        w_be = jnp.sum(topk_w[..., None] * onehot, axis=1)
        mask = np.ones((E, L), dtype=np.float32)
        mask[1, L_head:L_head + L_wrist] = 0.0
        mask[2, :L_head] = 0.0
        mask = jnp.asarray(mask)
        out = jnp.zeros_like(context_c)
        for e in range(E):
            h = jax.nn.gelu(context_c @ ew1[e] + eb1[e], approximate=True)
            y = h @ ew2[e] + eb2[e]
            out = out + w_be[:, e][:, None, None] * mask[e][None, :, None] * y
        shared = jax.nn.gelu(context_c @ sw1 + sb1, approximate=True) @ sw2 + sb2
        return out + shared

    def _L1_cond_ref(video, seq, W_z, U_z, C_z, b_z, W_r, U_r, C_r, b_r, W, U, C, b):
        import jax, jax.numpy as jnp
        import numpy as np
        B, T, D_IN, V_IN, E = (64, 128, 256, 256, 256)
        vz = video @ C_z + b_z
        vr = video @ C_r + b_r
        vh = video @ C + b
        xz = jnp.einsum('btd,de->bte', seq, W_z)
        xr = jnp.einsum('btd,de->bte', seq, W_r)
        xh = jnp.einsum('btd,de->bte', seq, W)

        def step(h, xs):
            xzt, xrt, xht = xs
            z = jax.nn.sigmoid(xzt + h @ U_z + vz)
            r = jax.nn.sigmoid(xrt + h @ U_r + vr)
            hh = jnp.tanh(xht + r * h @ U + vh)
            h_new = (1.0 - z) * h + z * hh
            return (h_new, h_new)
        h0 = jnp.zeros((seq.shape[0], U.shape[0]), seq.dtype)
        xs = (jnp.swapaxes(xz, 0, 1), jnp.swapaxes(xr, 0, 1), jnp.swapaxes(xh, 0, 1))
        _, out_t = jax.lax.scan(step, h0, xs)
        return jnp.swapaxes(out_t, 0, 1)
    x = x + _L0_cond_ref(x, cond_1024, L0_cond_gate_w, L0_cond_gate_b, L0_cond_time_w, L0_cond_time_b, L0_cond_ew1, L0_cond_eb1, L0_cond_ew2, L0_cond_eb2, L0_cond_sw1, L0_cond_sb1, L0_cond_sw2, L0_cond_sb2)
    x = x + _L1_cond_ref(cond_1024, x, L1_cond_W_z, L1_cond_U_z, L1_cond_C_z, L1_cond_b_z, L1_cond_W_r, L1_cond_U_r, L1_cond_C_r, L1_cond_b_r, L1_cond_W, L1_cond_U, L1_cond_C, L1_cond_b)
    return x

_drawn_inputs = setup_inputs


def setup_inputs(seed=0):
    import zlib

    import numpy as np

    out = dict(_drawn_inputs(seed))
    spreads = {'L0_cond_gate_b': (0.0, 2.0),
     'L0_cond_time_b': (0.0, 0.8),
     'L0_cond_eb1': (0.0, 0.371),
     'L0_cond_eb2': (0.0, 0.1),
     'L0_cond_sb1': (0.0, 0.1),
     'L0_cond_sb2': (0.0, 0.1),
     'L1_cond_b_z': (0.0, 2.0),
     'L1_cond_b_r': (0.0, 2.0),
     'L1_cond_b': (0.0, 0.1)}
    factors = {'L0_cond_gate_w': 64.0,
     'L1_cond_W_z': 7.171,
     'L1_cond_U_z': 43.974,
     'L1_cond_C_z': 8.0,
     'L1_cond_W_r': 23.462,
     'L1_cond_U_r': 64.0,
     'L1_cond_C_r': 27.024,
     'L1_cond_U': 4.077,
     'L0_cond_time_w': 5.751}
    for name, (base, spread) in spreads.items():
        noise = np.random.default_rng([zlib.crc32(name.encode()), seed]).standard_normal(out[name].shape)
        drawn = base * np.exp(spread * noise) if base else spread * noise
        out[name] = jnp.asarray(drawn.astype(out[name].dtype))
    for name, factor in factors.items():
        out[name] = (out[name] * factor).astype(out[name].dtype)
    return out
```

```python
from contextlib import ExitStack

import numpy as np

import concourse.bass as bass
from concourse import mybir

ALU = mybir.AluOpType
ACT = mybir.ActivationFunctionType
AX = mybir.AxisListType
F32 = mybir.dt.float32
F16 = mybir.dt.float16
BF16 = mybir.dt.bfloat16
I32 = mybir.dt.int32

P = 128
GATES = 3
R, Z, C = range(GATES)
STEPS = 16
LOW = 1024.0
PLOW = 2048.0
FILL = 28


def moe_gru_kernel(nc, x, cond, gate_w, gate_b, time_w, time_b, ew1, eb1, ew2, eb2, sw1, sb1, sw2, sb2,
                   w_z, u_z, c_z, b_z, w_r, u_r, c_r, b_r, w_h, u_h, c_h, b_h, branch_mask, out):
    B, T, D = x.shape
    E, _, H = ew1.shape
    BR = E + 1
    KC = D // P
    TC = P
    CH = T // TC
    COLS = TC * B
    HALF = COLS // 2
    BODIES = TC // STEPS
    HT = H // P
    SC = STEPS * B
    ST = KC * B
    THIRD = T // 3
    assert HT == BODIES and KC == 2 and B == 2 and D == 2 * P

    w_in = [w_r, w_z, w_h]
    u_in = [u_r, u_z, u_h]
    c_in = [c_r, c_z, c_h]
    b_in = [b_r, b_z, b_h]

    ROW_B1, ROW_BG, ROW_COND = 0, BR * HT, BR * HT + GATES * KC
    ROWS = ROW_COND + B * KC

    ctx = ExitStack()
    with ctx:
        def sb(name, shape, dt=F32):
            return ctx.enter_context(nc.sbuf_tensor(name, shape, dt))

        def pb(name):
            return ctx.enter_context(nc.psum_tensor(name, [P, 512], F32))

        def sem(name):
            return ctx.enter_context(nc.semaphore(name))

        x_rows = sb("x_rows", [P, CH, B, D])
        feat = sb("feat", [P, KC, T * B])
        gate_scale = sb("gate_scale", [P, 2, T * B])
        expert_w = sb("expert_w", [P, BR, B])
        branch_rows = sb("branch_rows", [BR, T * B])
        mask_rows = sb("mask_rows", [BR, T])
        bias2_rows = sb("bias2_rows", [BR, D])
        up_w = sb("up_w", [P, BR, KC, P])
        down_w = sb("down_w", [P, BR, D])
        hidden = sb("hidden", [P, 2, COLS])
        bias1_now = sb("bias1_now", [P, BR])
        small_rows = sb("small_rows", [P, P])
        small_cols = sb("small_cols", [P, ROWS])
        wx = sb("wx", [P, GATES, KC, D])
        uf = sb("uf", [P, GATES, KC, D])
        cf = sb("cf", [P, GATES, KC, D])
        u_high = sb("u_high", [P, GATES, KC, D], F16)
        u_mid = sb("u_mid", [P, GATES, KC, D], F16)
        u_low = sb("u_low", [P, GATES, KC, D], F16)
        gate_bias = sb("gate_bias", [P, GATES, KC, B])
        xpart = sb("xpart", [P, GATES * KC, COLS])
        xrest = sb("xrest", [P, GATES * KC, SC])
        xsplit = sb("xsplit", [P, 3, GATES * KC, SC], BF16)
        h_body = sb("h_body", [P, KC, SC])
        out_feat = sb("out_feat", [P, KC, COLS])
        out_rows = sb("out_rows", [P, B * D])
        ident = sb("ident", [P, P])
        ident16 = sb("ident16", [P, P], BF16)
        ones = sb("ones", [P, P])
        gate_w_sb = sb("gate_w_sb", [P, 3, KC, E])
        time_w_sb = sb("time_w_sb", [P, KC, 2 * E])
        bias_row = sb("bias_row", [1, 3 * E])
        umax = sb("umax", [P, GATES])
        uall = sb("uall", [P, GATES])
        upow = sb("upow", [P, GATES])
        act_scale = sb("act_scale", [P, GATES])
        seg_sum = sb("seg_sum", [P, 3, KC * B])
        agg = sb("agg", [P, 3, KC, B])
        cond_tanh = sb("cond_tanh", [P, B * KC])
        cond_silu = sb("cond_silu", [P, B * KC])
        modul = sb("modul", [B, 2 * E])
        logit = sb("logit", [B, E])
        small = sb("small", [B, 8])
        score = sb("score", [B, E])
        above = sb("above", [B, E, E])
        equal = sb("equal", [B, E, E])
        before = sb("before", [B, E, E])
        rank = sb("rank", [B, E])
        picked = sb("picked", [B, BR])
        spread = sb("spread", [B, BR, B])

        parts = sb("parts", [P, 8, KC, FILL], F16)
        P_HI, P_LO, A_HI, A_LO, Q_HI, Q_LO, H_HI, H_LO = range(8)
        tanh_out = sb("tanh_out", [P, GATES, ST])
        st = sb("st", [P, 9, ST])
        PP, V, VV, A, AA, ZZ, QQ, HK, HH = range(9)

        gate_ps = [pb("r_ps"), pb("z_ps"), pb("c_ps")]
        up_ps = [pb("up0_ps"), pb("up1_ps")]
        y_ps = pb("y_ps")
        xp_ps = [pb("xp0_ps"), pb("xp1_ps")]
        rows_ps = xp_ps[1]
        gate_v = [g[:, 0:KC * SC].rearrange("p (m s b) -> p m s b", m=KC, b=B) for g in gate_ps]

        x_in = [sem(f"x_in{i}") for i in range(CH)]
        small_in = sem("small_in")
        mats_in = sem("mats_in")
        ident_made = sem("ident_made")
        pool_chain = sem("pool_chain")
        pool_passed = sem("pool_passed")
        x_turned = sem("x_turned")
        x_copied = sem("x_copied")
        rows_turned = sem("rows_turned")
        cols_copied = sem("cols_copied")
        umax_local = sem("umax_local")
        umax_shared = sem("umax_shared")
        setup_chain = sem("setup_chain")
        gbias_summed = sem("gbias_summed")
        silu_tanh = sem("silu_tanh")
        silu_made = sem("silu_made")
        agg_made = sem("agg_made")
        logits_made = sem("logits_made")
        logits_shifted = sem("logits_shifted")
        exp_made = sem("exp_made")
        spread_made = sem("spread_made")
        weights_shared = sem("weights_shared")
        scales_made = sem("scales_made")
        up_in = [sem(f"up_in{e}") for e in range(BR)]
        down_in = [sem(f"down_in{e}") for e in range(BR)]
        up_done = sem("up_done")
        down_done = sem("down_done")
        gelu_done = sem("gelu_done")
        scaled = sem("scaled")
        bias1_ready = sem("bias1_ready")
        feat_ready = sem("feat_ready")
        xp_done = sem("xp_done")
        xp_ready = sem("xp_ready")
        split_ready = sem("split_ready")
        injected = sem("injected")
        preact = sem("preact")
        act_done = sem("act_done")
        part_ready = sem("part_ready")
        state = sem("state")
        body_h = sem("body_h")
        body_added = sem("body_added")
        turned = sem("turned")
        turned_copied = sem("turned_copied")
        out_written = sem("out_written")

        PARTS_STEP, STATE_STEP = 8, 9
        block = ctx.enter_context(nc.Block())

        @block.sync
        def _(sp):
            for i in range(CH):
                sp.dma_start(x_rows[:, i, :, :],
                             x[:, i * P:(i + 1) * P, :].rearrange("b p d -> p b d")).then_inc(x_in[i], 16)
            sp.sem_inc(up_done, BR)
            sp.sem_inc(down_done, BR)
            with sp.Fori(0, CH) as c:
                with sp.Fori(0, BODIES) as j:
                    units = c * (BODIES * BR) + j * BR
                    for e in range(BR):
                        w1 = ew1[e, :, :] if e < E else sw1
                        w2 = ew2[e, :, :] if e < E else sw2
                        sp.wait_ge(up_done, units + (e + 1))
                        sp.dma_start(up_w[:, e, :, :],
                                     w1.rearrange("(k p) n -> p k n", p=P)[:, :, bass.ds(j * P, P)]
                                     ).then_inc(up_in[e], 16)
                        sp.wait_ge(down_done, units + (e + 1))
                        sp.dma_start(down_w[:, e, :], w2[bass.ds(j * P, P), :]).then_inc(down_in[e], 16)

        @block.gpsimd
        def _(pool):
            pool.memset(ones[:, :], 1.0).then_inc(ident_made, 1)
            pool.memset(ident[:, :], 0.0).then_inc(pool_chain, 1)
            pool.wait_ge(pool_chain, 1)
            pool.affine_select(out=ident[:, :], in_=ident[:, :], compare_op=ALU.not_equal, fill=1.0,
                               base=0, pattern=[[-1, P]], channel_multiplier=1).then_inc(ident_made, 1)
            pool.wait_ge(ident_made, 2)
            pool.tensor_copy(ident16[:, :], ident[:, :]).then_inc(ident_made, 1)
            pool.wait_ge(umax_local, 1)
            pool.partition_all_reduce(uall[:, :], umax[:, :], P,
                                      bass.bass_isa.ReduceOp.max).then_inc(umax_shared, 1)
            pool.sem_inc(split_ready, 1)
            pool.sem_inc(body_added, 1)
            CHAIN0, PER_SPLIT = 1, 3

            def wait_apart(semaphore, value):
                pool.wait_ge(semaphore, value)
                pool.sem_inc(pool_passed, 1)

            def split(c, j):
                n = c * BODIES + j
                chain = n * PER_SPLIT + CHAIN0
                src = xpart[:, :, bass.ds(j * SC, SC)]
                if isinstance(j, int) and j == 0:
                    pool.wait_ge(xp_ready, (c + 1) * GATES + 1)
                wait_apart(injected, n + 1)
                pool.tensor_copy(xsplit[:, 0, :, :], src).then_inc(pool_chain, 1)
                wait_apart(pool_chain, chain + 1)
                pool.tensor_tensor(xrest[:, :, :], src, xsplit[:, 0, :, :],
                                   ALU.subtract).then_inc(pool_chain, 1)
                wait_apart(pool_chain, chain + 2)
                pool.tensor_copy(xsplit[:, 1, :, :], xrest[:, :, :]).then_inc(pool_chain, 1)
                pool.wait_ge(pool_chain, chain + 3)
                pool.tensor_tensor(xsplit[:, 2, :, :], xrest[:, :, :], xsplit[:, 1, :, :],
                                   ALU.subtract).then_inc(split_ready, 1)

            def add_body(c, j):
                n = c * BODIES + j
                pool.wait_ge(body_h, n + 1)
                wait_apart(turned, c + 1)
                pool.tensor_tensor(out_feat[:, :, bass.ds(j * SC, SC)], h_body[:, :, :],
                                   feat[:, :, bass.ds(c * COLS + j * SC, SC)], ALU.add
                                   ).then_inc(body_added, 1)

            with pool.Fori(0, CH) as c:
                split(c, 0)
                with pool.Fori(0, BODIES - 1) as j:
                    split(c, j + 1)
                    add_body(c, j)
                add_body(c, BODIES - 1)

        @block.scalar
        def _(act):
            b1_rows = eb1.rearrange("e (t p) -> e t p", p=P)
            small_count = 0
            for e in range(BR):
                src = b1_rows[e, :, :] if e < E else sb1.rearrange("(t p) -> t p", p=P)
                act.dma_start(small_rows[ROW_B1 + e * HT:ROW_B1 + (e + 1) * HT, :], src).then_inc(small_in, 16)
            for g in range(GATES):
                act.dma_start(small_rows[ROW_BG + g * KC:ROW_BG + (g + 1) * KC, :],
                              b_in[g].rearrange("(k p) -> k p", p=P)).then_inc(small_in, 16)
            act.dma_start(small_rows[ROW_COND:ROW_COND + B * KC, :],
                          cond.rearrange("b (k p) -> (b k) p", p=P)).then_inc(small_in, 16)
            for g in range(GATES):
                act.dma_start(uf[:, g, :, :], u_in[g].rearrange("(k p) n -> p k n", p=P)).then_inc(mats_in, 16)
                act.dma_start(wx[:, g, :, :], w_in[g].rearrange("(k p) n -> p k n", p=P)).then_inc(mats_in, 16)
                act.dma_start(cf[:, g, :, :], c_in[g].rearrange("(k p) n -> p k n", p=P)).then_inc(mats_in, 16)
            act.dma_start(gate_w_sb[:, :, :, :], gate_w.rearrange("(s k p) n -> p s k n", p=P, k=KC)).then_inc(mats_in, 16)
            act.dma_start(time_w_sb[:, :, :], time_w.rearrange("(k p) n -> p k n", p=P)).then_inc(mats_in, 16)
            act.dma_start(bias_row[:, 0:2 * E], time_b.rearrange("(a n) -> a n", a=1)).then_inc(mats_in, 16)
            act.dma_start(bias_row[:, 2 * E:3 * E], gate_b.rearrange("(a n) -> a n", a=1)).then_inc(mats_in, 16)
            act.dma_start(bias2_rows[0:E, :], eb2).then_inc(mats_in, 16)
            act.dma_start(bias2_rows[E:BR, :], sb2.rearrange("(a n) -> a n", a=1)).then_inc(mats_in, 16)
            act.dma_start(mask_rows[:, :], branch_mask).then_inc(mats_in, 16)

            act.sem_inc(gelu_done, 1)
            act.sem_inc(turned_copied, 1)
            act.sem_inc(out_written, 16)

            act.wait_ge(cols_copied, 1)
            act.activation(cond_tanh[:, :], small_cols[:, ROW_COND:ROW_COND + B * KC], ACT.Tanh,
                           scale=0.5).then_inc(silu_tanh, 1)
            act.wait_ge(logits_shifted, 1)
            act.activation(score[:, :], logit[:, :], ACT.Exp).then_inc(exp_made, 1)

            def gelu_half(c, j, e, half):
                units = (c * BODIES + j) * BR
                if half == 0:
                    if e == 0:
                        act.wait_ge(bias1_ready, c * BODIES + j + 1)
                    act.wait_ge(up_done, units + (BR + e + 1))
                    if e != 1:
                        act.wait_ge(down_done, units + (BR if e == 0 else BR + e - 1))
                cols = slice(half * HALF, (half + 1) * HALF)
                act.activation(hidden[:, e % 2, cols], up_ps[e % 2][:, cols], ACT.Gelu_apprx_tanh,
                               bias=bias1_now[:, e:e + 1]).then_inc(gelu_done, 1)

            def gate_tanh(t, g):
                act.wait_ge(preact, t * GATES + g + 1)
                act.activation(tanh_out[:, g, :].rearrange("p (m b) -> p m b", b=B),
                               gate_v[g][:, :, t, :], ACT.Tanh,
                               scale=act_scale[:, g:g + 1]).then_inc(act_done, 1)

            def gru_body(c, j, with_ffn):
                for t in range(STEPS):
                    gate_tanh(t, R)
                    gate_tanh(t, Z)
                    gate_tanh(t, C)
                    e, phase = divmod(t, 3)
                    if with_ffn and e < BR and phase < 2:
                        gelu_half(c + 1, j, e, phase)
                act.drain()
                act.sem_inc(preact, -STEPS * GATES)

            def write_chunk(c):
                act.wait_ge(turned, c + 2)
                act.wait_ge(out_written, c * 16 + 16)
                act.activation(out_rows[:, :], rows_ps[:, :], ACT.Copy).then_inc(turned_copied, 1)
                act.wait_ge(turned_copied, c + 2)
                act.dma_start(out[:, bass.ds(c * TC, TC), :].rearrange("b p d -> p b d"),
                              out_rows[:, :].rearrange("p (b d) -> p b d", b=B)).then_inc(out_written, 16)

            with act.Fori(0, BODIES) as j:
                for e in range(BR):
                    for half in range(2):
                        gelu_half(0, j, e, half)
            with act.Fori(0, CH - 1) as c:
                with act.Fori(0, BODIES) as j:
                    gru_body(c, j, True)
                write_chunk(c)
            with act.Fori(0, BODIES) as j:
                gru_body(CH - 1, j, False)
            write_chunk(CH - 1)
            act.wait_ge(out_written, CH * 16 + 16)

        @block.vector
        def _(dve):
            chain = [0]
            dve.sem_inc(xp_ready, 1)

            def link(ins):
                chain[0] += 1
                ins.then_inc(setup_chain, 1)
                dve.wait_ge(setup_chain, chain[0])

            dve.memset(before[:, :, :], 0.0)
            dve.memset(parts[:, :, :, :], 0.0).then_inc(part_ready, PARTS_STEP)
            dve.memset(h_body[:, :, :], 0.0)
            link(dve.memset(picked[:, :], 1.0))
            dve.memset(st[:, :, :], 0.0).then_inc(state, STATE_STEP)
            for e in range(1, E):
                dve.memset(before[:, e, 0:e], 1.0)
            link(dve.memset(gate_scale[:, :, :], 0.0))

            dve.wait_ge(rows_turned, 1)
            dve.tensor_copy(small_cols[:, :], y_ps[:, 0:ROWS]).then_inc(cols_copied, 1)

            for i in range(CH):
                dve.wait_ge(x_turned, i + 1)
                dve.tensor_copy(feat[:, :, i * COLS:(i + 1) * COLS].rearrange("p k (t b) -> p k b t", b=B),
                                xp_ps[i % 2][:, :].rearrange("p (k b t) -> p k b t", k=KC, b=B)
                                ).then_inc(x_copied, 1)
            dve.wait_ge(x_copied, CH)

            dve.wait_ge(mats_in, 16 * 16)
            link(dve.tensor_reduce(umax[:, :], uf[:, :, :, :].rearrange("p g k n -> p g (k n)"), AX.X,
                                   ALU.max, apply_absolute_value=True))
            dve.tensor_scalar(umax[:, :], umax[:, :], 2.0 ** -100, None, ALU.max).then_inc(umax_local, 1)
            dve.wait_ge(umax_shared, 1)
            link(dve.tensor_scalar(upow[:, :].bitcast(I32), uall[:, :].bitcast(I32), 0x7F800000, None,
                                   ALU.bitwise_and))
            link(dve.reciprocal(upow[:, :], upow[:, :]))
            link(dve.tensor_scalar(upow[:, :], upow[:, :], 2.0 ** 14, 4096.0, ALU.mult, ALU.min))
            link(dve.reciprocal(act_scale[:, :], upow[:, :]))
            link(dve.tensor_scalar(act_scale[:, 0:2], act_scale[:, 0:2], 0.5, None, ALU.mult))
            for g in range(GATES):
                for m in (uf, wx):
                    last = dve.tensor_scalar(m[:, g, :, :], m[:, g, :, :], upow[:, g:g + 1], None, ALU.mult)
            link(last)
            link(dve.tensor_copy(u_high[:, :, :, :], uf[:, :, :, :]))
            for g in range(GATES):
                dve.tensor_tensor(u_mid[:, g, :, :], uf[:, g, :, :], u_high[:, g, :, :], ALU.subtract)
                last = dve.tensor_scalar(u_low[:, g, :, :], u_high[:, g, :, :],
                                         1.0 / (PLOW if g == C else LOW), None, ALU.mult)
            link(last)

            dve.wait_ge(gbias_summed, 1)
            gb = y_ps[:, 0:GATES * KC * B].rearrange("p (g k b) -> p (g k) b", k=KC, b=B)
            bg = small_cols[:, ROW_BG:ROW_BG + GATES * KC].unsqueeze(2).broadcast_to([P, GATES * KC, B])
            link(dve.tensor_tensor(gate_bias[:, :, :, :].rearrange("p g k b -> p (g k) b"), gb, bg, ALU.add))
            for g in range(GATES):
                last = dve.tensor_scalar(gate_bias[:, g, :, :], gate_bias[:, g, :, :], upow[:, g:g + 1], None,
                                         ALU.mult)
            link(last)

            dve.wait_ge(silu_tanh, 1)
            link(dve.scalar_tensor_tensor(cond_silu[:, :], cond_tanh[:, :], 1.0,
                                          small_cols[:, ROW_COND:ROW_COND + B * KC], ALU.add, ALU.mult))
            dve.tensor_scalar(cond_silu[:, :], cond_silu[:, :], 0.5, None, ALU.mult).then_inc(silu_made, 1)

            for s, (lo, hi) in enumerate(((0, THIRD), (THIRD, 2 * THIRD), (2 * THIRD, T))):
                last = dve.tensor_reduce(
                    seg_sum[:, s, :].rearrange("p (k b) -> p k b", b=B),
                    feat[:, :, lo * B:hi * B].rearrange("p k (t b) -> p k b t", b=B), AX.X, ALU.add)
            link(last)
            flat = agg[:, :, :, :].rearrange("p s k b -> p s (k b)")
            dve.tensor_tensor(flat[:, 1, :], seg_sum[:, 0, :], seg_sum[:, 2, :], ALU.add)
            link(dve.tensor_tensor(flat[:, 2, :], seg_sum[:, 1, :], seg_sum[:, 2, :], ALU.add))
            link(dve.tensor_tensor(flat[:, 0, :], flat[:, 1, :], seg_sum[:, 1, :], ALU.add))
            dve.tensor_scalar(flat[:, 0, :], flat[:, 0, :], 1.0 / T, None, ALU.mult)
            dve.tensor_scalar(flat[:, 1:3, :], flat[:, 1:3, :], 1.0 / (T - THIRD), None,
                              ALU.mult).then_inc(agg_made, 1)

            dve.wait_ge(logits_made, 1)
            link(dve.tensor_copy(modul[:, :], y_ps[0:B, 0:2 * E]))
            link(dve.tensor_scalar(modul[:, 0:E], modul[:, 0:E], 1.0, None, ALU.add))
            link(dve.tensor_tensor(logit[:, :], y_ps[0:B, 2 * E:3 * E], modul[:, 0:E], ALU.mult))
            link(dve.tensor_tensor(logit[:, :], logit[:, :], modul[:, E:2 * E], ALU.add))
            link(dve.tensor_reduce(small[:, 0:1], logit[:, :], AX.X, ALU.max))
            dve.tensor_scalar(logit[:, :], logit[:, :], small[:, 0:1], None, ALU.subtract
                              ).then_inc(logits_shifted, 1)
            dve.wait_ge(exp_made, 1)
            link(dve.tensor_reduce(small[:, 1:2], score[:, :], AX.X, ALU.add))
            link(dve.reciprocal(small[:, 2:3], small[:, 1:2]))
            link(dve.tensor_scalar(score[:, :], score[:, :], small[:, 2:3], None, ALU.mult))

            s_j = score[:, :].unsqueeze(1).broadcast_to([B, E, E])
            s_e = score[:, :].unsqueeze(2).broadcast_to([B, E, E])
            dve.tensor_tensor(above[:, :, :], s_j, s_e, ALU.is_gt)
            link(dve.tensor_tensor(equal[:, :, :], s_j, s_e, ALU.is_equal))
            link(dve.tensor_tensor(equal[:, :, :], equal[:, :, :], before[:, :, :], ALU.mult))
            link(dve.tensor_tensor(above[:, :, :], above[:, :, :], equal[:, :, :], ALU.add))
            link(dve.tensor_reduce(rank[:, :], above[:, :, :], AX.X, ALU.add))
            link(dve.scalar_tensor_tensor(picked[:, 0:E], rank[:, :], 1.5, score[:, :], ALU.is_lt, ALU.mult))
            link(dve.tensor_reduce(small[:, 3:4], picked[:, 0:E], AX.X, ALU.add))
            link(dve.tensor_scalar(small[:, 3:4], small[:, 3:4], 1e-8, None, ALU.add))
            link(dve.reciprocal(small[:, 4:5], small[:, 3:4]))
            link(dve.tensor_scalar(picked[:, 0:E], picked[:, 0:E], small[:, 4:5], None, ALU.mult))
            dve.tensor_tensor(spread[:, :, :], picked[:, :].unsqueeze(2).broadcast_to([B, BR, B]),
                              ident[0:B, 0:B].unsqueeze(1).broadcast_to([B, BR, B]), ALU.mult
                              ).then_inc(spread_made, 1)
            dve.wait_ge(weights_shared, 1)
            link(dve.tensor_copy(expert_w[:, :, :].rearrange("p e b -> p (e b)"), y_ps[:, 0:BR * B]))
            wide = gate_scale[:, :, :].rearrange("p e (t b) -> p e t b", b=B)
            for row, e, lo, hi in ((0, 1, 0, THIRD), (0, 1, 2 * THIRD, T), (1, 2, THIRD, T)):
                dve.tensor_copy(wide[:, row, lo:hi, :],
                                expert_w[:, e, :].unsqueeze(1).broadcast_to([P, hi - lo, B]))
            dve.tensor_tensor(branch_rows[:, :].rearrange("e (t b) -> e t b", b=B),
                              mask_rows[:, :].unsqueeze(2).broadcast_to([BR, T, B]),
                              y_ps[0:BR, 16:16 + B].unsqueeze(1).broadcast_to([BR, T, B]), ALU.mult
                              ).then_inc(scales_made, 1)
            dve.wait_ge(scales_made, 1)

            def bias1(c, j):
                dve.wait_ge(gelu_done, (c * BODIES + j) * (2 * BR) + 1)
                src = small_cols[:, 0:BR * HT].rearrange("p (e t) -> p e t", e=BR)
                dve.tensor_scalar(bias1_now[:, :].unsqueeze(2), src[:, :, bass.ds(j, 1)], 1.0, None,
                                  ALU.mult).then_inc(bias1_ready, 1)

            def scale_half(c, j, e, half):
                dve.wait_ge(gelu_done, (c * BODIES + j) * (2 * BR) + (2 * e + half + 2))
                cols = hidden[:, e % 2, half * HALF:(half + 1) * HALF]
                if e in (1, 2):
                    w = gate_scale[:, e - 1, bass.ds(c * COLS + half * HALF, HALF)]
                    dve.tensor_tensor(cols, cols, w, ALU.mult).then_inc(scaled, 1)
                else:
                    v = cols.rearrange("p (t b) -> p t b", b=B)
                    w = expert_w[:, e, :].unsqueeze(1).broadcast_to([P, HALF // B, B])
                    dve.tensor_tensor(v, v, w, ALU.mult).then_inc(scaled, 1)

            def chunk_tail(c):
                dve.wait_ge(down_done, (c + 1) * (BODIES * BR) + BR)
                here = feat[:, :, bass.ds(c * COLS, COLS)]
                dve.tensor_tensor(here, y_ps[:, :].rearrange("p (k n) -> p k n", k=KC), here, ALU.add
                                  ).then_inc(feat_ready, 1)
                for g in range(GATES):
                    dve.wait_ge(xp_done, c * GATES + (g + 1))
                    if g == 0:
                        dve.wait_ge(split_ready, c * BODIES + 1)
                    dve.tensor_tensor(
                        xpart[:, g * KC:(g + 1) * KC, :].rearrange("p k (t b) -> p k t b", b=B),
                        xp_ps[g % 2][:, :].rearrange("p (k t b) -> p k t b", k=KC, b=B),
                        gate_bias[:, g, :, :].unsqueeze(2).broadcast_to([P, KC, TC, B]), ALU.add
                    ).then_inc(xp_ready, 1)

            def gru_body(c, j, with_ffn):
                n = c * BODIES + j
                for t in range(STEPS):
                    gate0 = t * GATES
                    s0 = (t + 1) * STATE_STEP
                    tr, tz, tc = (tanh_out[:, g, :].rearrange("p (m b) -> p m b", b=B) for g in range(GATES))
                    now = h_body[:, :, t * B:(t + 1) * B]
                    prev_t = (t - 1) % STEPS
                    prev = h_body[:, :, prev_t * B:(prev_t + 1) * B]
                    sq = lambda ap: ap.rearrange("p (m b) -> p m b", b=B)
                    s = lambda i: sq(st[:, i, :])
                    p = lambda i: parts[:, i, :, 0:B]

                    dve.wait_ge(act_done, gate0 + 1)
                    dve.wait_ge(state, s0)
                    dve.scalar_tensor_tensor(p(P_HI), tr, 1.0, s(HH), ALU.add, ALU.mult).then_inc(part_ready, 1)
                    dve.scalar_tensor_tensor(s(PP), tr, 1.0, s(HK), ALU.add, ALU.mult).then_inc(state, 1)
                    dve.wait_ge(state, s0 + 1)
                    dve.scalar_tensor_tensor(p(P_LO), p(P_HI), -PLOW, s(PP), ALU.mult, ALU.add
                                             ).then_inc(part_ready, 1)
                    if with_ffn and t == 0:
                        bias1(c + 1, j)

                    dve.wait_ge(act_done, gate0 + 2)
                    dve.scalar_tensor_tensor(s(VV), tz, 1.0, s(HK), ALU.add, ALU.mult).then_inc(state, 1)
                    dve.scalar_tensor_tensor(s(V), tz, 1.0, s(HH), ALU.add, ALU.mult).then_inc(state, 1)
                    dve.tensor_scalar(s(ZZ), tz, 1.0, 0.5, ALU.add, ALU.mult).then_inc(state, 1)
                    dve.wait_ge(state, s0 + 3)
                    dve.tensor_tensor(p(A_HI), prev, s(V), ALU.subtract).then_inc(part_ready, 1)
                    dve.scalar_tensor_tensor(s(AA), s(VV), -LOW / PLOW, s(HK), ALU.mult, ALU.add
                                             ).then_inc(state, 1)
                    dve.tensor_tensor(s(A), prev, s(V), ALU.subtract).then_inc(state, 1)
                    dve.wait_ge(state, s0 + 5)
                    dve.scalar_tensor_tensor(p(A_LO), p(A_HI), -LOW, s(AA), ALU.mult, ALU.add
                                             ).then_inc(part_ready, 1)

                    dve.wait_ge(act_done, gate0 + 3)
                    dve.tensor_tensor(p(Q_HI), s(ZZ), tc, ALU.mult).then_inc(part_ready, 1)
                    dve.scalar_tensor_tensor(s(QQ), tc, LOW, s(ZZ), ALU.mult, ALU.mult).then_inc(state, 1)
                    dve.wait_ge(state, s0 + 7)
                    dve.scalar_tensor_tensor(p(Q_LO), p(Q_HI), -LOW, s(QQ), ALU.mult, ALU.add
                                             ).then_inc(part_ready, 1)
                    dve.scalar_tensor_tensor(p(H_HI), s(QQ), 1.0 / LOW, s(A), ALU.mult, ALU.add
                                             ).then_inc(part_ready, 1)
                    dve.tensor_tensor(s(HK), s(QQ), s(AA), ALU.add).then_inc(state, 1)
                    if t == 0:
                        dve.wait_ge(body_added, n + 1)
                    last_h = dve.scalar_tensor_tensor(now, s(QQ), 1.0 / LOW, s(A), ALU.mult, ALU.add)
                    if t == STEPS - 1:
                        last_h.then_inc(body_h, 1)
                    dve.wait_ge(state, s0 + 8)
                    dve.scalar_tensor_tensor(p(H_LO), p(H_HI), -LOW, s(HK), ALU.mult, ALU.add
                                             ).then_inc(part_ready, 1)
                    dve.tensor_scalar(s(HH), s(HK), 0.5 / LOW, None, ALU.mult).then_inc(state, 1)
                    e, phase = divmod(t, 3)
                    if with_ffn and e < E and phase < 2:
                        scale_half(c + 1, j, e, phase)
                dve.drain()
                dve.sem_inc(act_done, -STEPS * GATES)
                dve.sem_inc(state, -STEPS * STATE_STEP)

            with dve.Fori(0, BODIES) as j:
                bias1(0, j)
                for e in range(E):
                    for half in range(2):
                        scale_half(0, j, e, half)
            chunk_tail(0)
            with dve.Fori(0, CH - 1) as c:
                with dve.Fori(0, BODIES) as j:
                    gru_body(c, j, True)
                chunk_tail(c + 1)
            with dve.Fori(0, BODIES) as j:
                gru_body(CH - 1, j, False)

        @block.tensor
        def _(pe):
            mm = pe.matmul

            pe.sem_inc(injected, 1)
            pe.sem_inc(turned, 1)

            pe.wait_ge(ident_made, 3)
            pe.wait_ge(small_in, 16 * (BR + GATES + 1))
            pe.transpose(y_ps[:, 0:ROWS], small_rows[0:ROWS, :], ident[0:ROWS, 0:ROWS]).then_inc(rows_turned, 1)

            for i in range(CH):
                pe.wait_ge(x_in[i], 16)
                if i >= 2:
                    pe.wait_ge(x_copied, i - 1)
                for k in range(KC):
                    for b in range(B):
                        at = (k * B + b) * P
                        last = pe.transpose(xp_ps[i % 2][:, at:at + P], x_rows[:, i, b, k * P:(k + 1) * P],
                                            ident[:, :])
                last.then_inc(x_turned, 1)

            pe.wait_ge(mats_in, 16 * 16)
            pe.wait_ge(cols_copied, 1)
            cond_v = small_cols[:, ROW_COND:ROW_COND + B * KC].rearrange("p (b k) -> p k b", k=KC)
            for g in range(GATES):
                for m in range(KC):
                    at = (g * KC + m) * B
                    for k in range(KC):
                        last = mm(y_ps[:, at:at + B], cf[:, g, k, m * P:(m + 1) * P], cond_v[:, k, :],
                                  start=(g == 0 and m == 0 and k == 0), stop=(k == KC - 1),
                                  skip_group_check=True)
            last.then_inc(gbias_summed, 1)

            pe.wait_ge(silu_made, 1)
            silu_v = cond_silu[:, :].rearrange("p (b k) -> p k b", k=KC)
            for k in range(KC):
                mm(y_ps[0:B, 0:2 * E], silu_v[:, k, :], time_w_sb[:, k, :], start=(k == 0), stop=False,
                   skip_group_check=True)
            mm(y_ps[0:B, 0:2 * E], ones[0:1, 0:B], bias_row[:, 0:2 * E], start=False, stop=True,
               skip_group_check=True)
            pe.wait_ge(agg_made, 1)
            for s in range(3):
                for k in range(KC):
                    mm(y_ps[0:B, 2 * E:3 * E], agg[:, s, k, :], gate_w_sb[:, s, k, :], start=False, stop=False,
                       skip_group_check=True)
            mm(y_ps[0:B, 2 * E:3 * E], ones[0:1, 0:B], bias_row[:, 2 * E:3 * E], start=False, stop=True,
               skip_group_check=True).then_inc(logits_made, 1)

            pe.wait_ge(spread_made, 1)
            mm(y_ps[:, 0:BR * B], ones[0:B, :], spread[:, :, :].rearrange("q e b -> q (e b)"),
               start=True, stop=True, skip_group_check=True)
            mm(y_ps[0:BR, 16:16 + B], picked[:, :], ident[0:B, 0:B], start=False, stop=True,
               skip_group_check=True).then_inc(weights_shared, 1)

            def output_bias(c):
                for m in range(KC):
                    mm(y_ps[:, m * COLS:(m + 1) * COLS], bias2_rows[:, m * P:(m + 1) * P],
                       branch_rows[:, bass.ds(c * COLS, COLS)],
                       start=(m == 0), stop=False, skip_group_check=True)

            def up(c, j, e, k):
                n = c * BODIES + j
                if k == 0:
                    pe.wait_ge(up_in[e], (n + 1) * 16)
                    if e != 1:
                        pe.wait_ge(gelu_done, n * (2 * BR) + (1 if e == 0 else 2 * e - 1))
                last = mm(up_ps[e % 2][:, 0:COLS], up_w[:, e, k, :], feat[:, k, bass.ds(c * COLS, COLS)],
                          start=(k == 0), stop=(k == KC - 1), skip_group_check=True)
                if k == KC - 1:
                    last.then_inc(up_done, 1)

            def down(c, j, e, m):
                n = c * BODIES + j
                if m == 0:
                    pe.wait_ge(down_in[e], (n + 1) * 16)
                    if e < E:
                        pe.wait_ge(scaled, n * (2 * E) + (2 * e + 2))
                    else:
                        pe.wait_ge(gelu_done, (n + 1) * (2 * BR) + 1)
                last = mm(y_ps[:, m * COLS:(m + 1) * COLS], down_w[:, e, m * P:(m + 1) * P], hidden[:, e % 2, :],
                          start=False, stop=(m == KC - 1), skip_group_check=True)
                if m == KC - 1:
                    last.then_inc(down_done, 1)

            def chunk_tail(c, written):
                pe.wait_ge(feat_ready, c + 1)
                for g in range(GATES):
                    if g == 0:
                        pe.wait_ge(xp_ready, c * GATES + 1)
                    elif g == 1:
                        if not isinstance(c, int):
                            pe.wait_ge(turned_copied, written + 1)
                    else:
                        pe.wait_ge(xp_ready, c * GATES + 2)
                    for m in range(KC):
                        for k in range(KC):
                            last = mm(xp_ps[g % 2][:, m * COLS:(m + 1) * COLS], wx[:, g, k, m * P:(m + 1) * P],
                                      feat[:, k, bass.ds(c * COLS, COLS)], start=(m == 0 and k == 0),
                                      stop=(k == KC - 1), skip_group_check=True)
                    last.then_inc(xp_done, 1)

            def turn_chunk(c, gates_out):
                pe.wait_ge(body_added, (c + 1) * BODIES + 1)
                pe.wait_ge(xp_ready, gates_out + 1)
                pe.wait_ge(turned_copied, c + 1)
                for b in range(B):
                    for k in range(KC):
                        at = b * D + k * P
                        last = pe.transpose(rows_ps[:, at:at + P],
                                            out_feat[:, k, :].rearrange("p (t b) -> p b t", b=B)[:, b, :],
                                            ident[:, :])
                last.then_inc(turned, 1)

            def inject(g, last_of_body):
                for i in range(3):
                    last = mm(gate_ps[g][:, 0:KC * SC], ident16[:, :],
                              xsplit[:, i, g * KC:(g + 1) * KC, :].rearrange("p k n -> p (k n)"),
                              start=(i == 0), stop=(i == 2), skip_group_check=True)
                if last_of_body:
                    last.then_inc(injected, 1)

            def recur(g, t, part, weights, stop=False):
                for m in range(KC):
                    for k in range(KC):
                        for i, w in enumerate(weights):
                            last = mm(gate_ps[g][:, m * SC + t * B:m * SC + t * B + FILL],
                                      w[:, g, k, m * P:(m + 1) * P], parts[:, part, k, :], start=False,
                                      stop=stop and k == KC - 1 and i == len(weights) - 1,
                                      skip_group_check=True)
                return last

            BOTH, DOWNED = (u_high, u_mid), (u_low,)

            def gru_body(c, j, with_ffn):
                n = c * BODIES + j
                for t in range(STEPS):
                    e, phase = divmod(t, 3)
                    ffn = with_ffn and e < BR
                    before_n = t * PARTS_STEP
                    if t == 0:
                        pe.wait_ge(split_ready, n + 2)
                        inject(R, False)
                    pe.wait_ge(part_ready, before_n + (A_HI + 1))
                    if t == 0:
                        inject(Z, False)
                    recur(R, t, A_HI, BOTH)
                    pe.wait_ge(part_ready, before_n + (A_LO + 1))
                    recur(R, t, A_LO, DOWNED)
                    pe.wait_ge(part_ready, before_n + (Q_HI + 1))
                    recur(R, t, Q_HI, BOTH)
                    pe.wait_ge(part_ready, before_n + (Q_LO + 1))
                    recur(R, t, Q_LO, DOWNED, stop=True).then_inc(preact, 1)
                    if t == 0:
                        inject(C, True)
                    pe.wait_ge(part_ready, before_n + (H_HI + 1))
                    recur(Z, t, H_HI, BOTH)
                    pe.wait_ge(part_ready, before_n + (H_LO + 1))
                    recur(Z, t, H_LO, DOWNED, stop=True).then_inc(preact, 1)
                    if ffn and phase == 0:
                        up(c + 1, j, e, 0)
                    if ffn and phase == 2:
                        down(c + 1, j, e, 0)
                    pe.wait_ge(part_ready, before_n + (PARTS_STEP + P_HI + 1))
                    recur(C, t, P_HI, BOTH)
                    pe.wait_ge(part_ready, before_n + (PARTS_STEP + P_LO + 1))
                    recur(C, t, P_LO, DOWNED, stop=True).then_inc(preact, 1)
                    if ffn and phase == 0:
                        up(c + 1, j, e, 1)
                    if ffn and phase == 2:
                        down(c + 1, j, e, 1)
                pe.drain()
                pe.sem_inc(part_ready, -STEPS * PARTS_STEP)

            pe.wait_ge(scales_made, 1)
            output_bias(0)
            with pe.Fori(0, BODIES) as j:
                for e in range(BR + 1):
                    for k in range(KC):
                        if e < BR:
                            up(0, j, e, k)
                    for m in range(KC):
                        if e > 0:
                            down(0, j, e - 1, m)
            chunk_tail(0, 0)
            with pe.Fori(0, CH - 1) as c:
                output_bias(c + 1)
                with pe.Fori(0, BODIES) as j:
                    gru_body(c, j, True)
                chunk_tail(c + 1, c)
                turn_chunk(c, (c + 1) * GATES + 2)
            with pe.Fori(0, BODIES) as j:
                gru_body(CH - 1, j, False)
            turn_chunk(CH - 1, CH * GATES)


_INS = ['x', 'cond_1024', 'L0_cond_gate_w', 'L0_cond_gate_b', 'L0_cond_time_w', 'L0_cond_time_b',
        'L0_cond_ew1', 'L0_cond_eb1', 'L0_cond_ew2', 'L0_cond_eb2', 'L0_cond_sw1', 'L0_cond_sb1',
        'L0_cond_sw2', 'L0_cond_sb2', 'L1_cond_W_z', 'L1_cond_U_z', 'L1_cond_C_z', 'L1_cond_b_z',
        'L1_cond_W_r', 'L1_cond_U_r', 'L1_cond_C_r', 'L1_cond_b_r', 'L1_cond_W', 'L1_cond_U',
        'L1_cond_C', 'L1_cond_b']


def kernel(**inputs):
    import concourse.bacc as bacc
    from concourse.bass_utils import run_bass_kernel_spmd

    nc = bacc.Bacc("TRN2", target_bir_lowering=False, num_devices=1)
    arrays = {f"in_{name}": np.ascontiguousarray(inputs[name]) for name in _INS}
    b, t, d = arrays["in_x"].shape
    branches = arrays["in_L0_cond_ew1"].shape[0] + 1
    mask = np.ones((branches, t), np.float32)
    mask[1, t // 3:2 * (t // 3)] = 0.0
    mask[2, :t // 3] = 0.0
    arrays["in_branch_mask"] = mask
    args = [nc.dram_tensor(name, a.shape, mybir.dt.from_np(a.dtype), kind="ExternalInput").ap()
            for name, a in arrays.items()]
    out = nc.dram_tensor("out", (b, t, d), F32, kind="ExternalOutput").ap()
    moe_gru_kernel(nc, *args, out)
    r = run_bass_kernel_spmd(nc, [arrays], core_ids=[0])
    return r.results[0]["out"]
```

```python
from contextlib import ExitStack

import numpy as np

import concourse.bass as bass
from concourse import mybir

ALU = mybir.AluOpType
ACT = mybir.ActivationFunctionType
AX = mybir.AxisListType
F32 = mybir.dt.float32
F16 = mybir.dt.float16
BF16 = mybir.dt.bfloat16
I32 = mybir.dt.int32

P = 128
GATES = 3
R, Z, C = range(GATES)
STEPS = 16
LOW = 1024.0
PLOW = 2048.0
FP16_MAX = 65504.0
LEAD = 9
FILL = 40


def moe_gru_kernel(nc, x, cond, gate_w, gate_b, time_w, time_b, ew1, eb1, ew2, eb2, sw1, sb1, sw2, sb2,
                   w_z, u_z, c_z, b_z, w_r, u_r, c_r, b_r, w_h, u_h, c_h, b_h, branch_mask, out):
    B, T, D = x.shape
    E, _, H = ew1.shape
    BR = E + 1
    KC = D // P
    TC = P
    CH = T // TC
    COLS = TC * B
    HALF = COLS // 2
    BODIES = TC // STEPS
    HT = H // P
    SC = STEPS * B
    ST = KC * B
    THIRD = T // 3
    assert HT == BODIES and KC == 2 and B == 2 and D == 2 * P

    w_in = [w_r, w_z, w_h]
    u_in = [u_r, u_z, u_h]
    c_in = [c_r, c_z, c_h]
    b_in = [b_r, b_z, b_h]

    UP, DOWN = "up", "down"
    order = [(UP, 0), (UP, 1)]
    for e in range(2, BR):
        order += [(DOWN, e - 2), (UP, e)]
    order += [(DOWN, BR - 2), (DOWN, BR - 1)]
    units = [(kind, e, unit) for kind, e in order for unit in range(4)]
    FFN_UNITS = {}
    for t in range(STEPS):
        for window in range(2):
            FFN_UNITS[t, window] = [units.pop(0) for _ in range(2 if t % 2 == 0 and window == 0 else 1)]
    assert not units
    GELU_STEPS = {t + window: e for (t, window), some in FFN_UNITS.items()
                  for kind, e, unit in some if kind == UP and unit == 3}
    products = [(g, m, k) for g in range(GATES) for m in range(KC) for k in range(KC)]
    windows = [(4, 1), (5, 0), (5, 1), (6, 0), (6, 1), (7, 0), (7, 1), (8, 0), (9, 1), (10, 0), (10, 1), (11, 0)]
    TAIL_PRODUCTS = {w: (p,) for w, p in zip(windows, products)}
    pieces = [(g, m, b) for g in range(GATES) for m in range(KC) for b in range(B)]
    TAIL_PIECES = {t: [] for t in (6, 7, 8, 9, 10, 11, 12, 13)}
    for t, p in zip((6, 6, 7, 8, 9, 9, 10, 10, 11, 12, 13, 13), pieces):
        TAIL_PIECES[t].append(p)

    ROW_B1, ROW_BG, ROW_COND = 0, BR * HT, BR * HT + GATES * KC
    ROWS = ROW_COND + B * KC

    ctx = ExitStack()
    with ctx:
        def sb(name, shape, dt=F32):
            return ctx.enter_context(nc.sbuf_tensor(name, shape, dt))

        def pb(name):
            return ctx.enter_context(nc.psum_tensor(name, [P, 512], F32))

        def sem(name):
            return ctx.enter_context(nc.semaphore(name))

        x_rows = sb("x_rows", [P, CH, B, D])
        feat = sb("feat", [P, KC, T * B])
        gate_scale = sb("gate_scale", [P, 2, T * B])
        expert_w = sb("expert_w", [P, BR, B])
        branch_rows = sb("branch_rows", [BR, T * B])
        mask_rows = sb("mask_rows", [BR, T])
        bias2_rows = sb("bias2_rows", [BR, D])
        up_w = sb("up_w", [P, BR, KC, P])
        down_w = sb("down_w", [P, BR, D])
        hidden = sb("hidden", [P, 2, COLS])
        bias1_now = sb("bias1_now", [P, BR])
        small_rows = sb("small_rows", [P, P])
        small_cols = sb("small_cols", [P, ROWS])
        wx = sb("wx", [P, GATES, KC, D])
        uf = sb("uf", [P, GATES, KC, D])
        cf = sb("cf", [P, GATES, KC, D])
        u_high = sb("u_high", [P, GATES, KC, D], F16)
        u_mid = sb("u_mid", [P, GATES, KC, D], F16)
        u_low = sb("u_low", [P, GATES, KC, D], F16)
        gate_bias = sb("gate_bias", [P, GATES, KC, B])
        xpart = sb("xpart", [P, GATES * KC, COLS])
        xrest = sb("xrest", [P, GATES * KC, SC])
        xsplit = sb("xsplit", [P, 3, GATES * KC, SC], BF16)
        h_body = sb("h_body", [P, KC, SC])
        h_true = sb("h_true", [P, KC, SC])
        out_feat = sb("out_feat", [P, KC, SC])
        out_rows = sb("out_rows", [SC, D])
        ident = sb("ident", [P, P])
        ident16 = sb("ident16", [P, P], BF16)
        ones = sb("ones", [P, P])
        gate_w_sb = sb("gate_w_sb", [P, 3, KC, E])
        time_w_sb = sb("time_w_sb", [P, KC, 2 * E])
        bias_row = sb("bias_row", [1, 3 * E])
        umax = sb("umax", [P, 1])
        uall = sb("uall", [P, 1])
        w_scale = sb("w_scale", [P, 1])
        h_scale = sb("h_scale", [P, 1])
        half_s = sb("half_s", [P, 1])
        seg_sum = sb("seg_sum", [P, 3, KC * B])
        agg = sb("agg", [P, 3, KC, B])
        cond_tanh = sb("cond_tanh", [P, B * KC])
        cond_silu = sb("cond_silu", [P, B * KC])
        modul = sb("modul", [B, 2 * E])
        logit = sb("logit", [B, E])
        small = sb("small", [B, 8])
        score = sb("score", [B, E])
        above = sb("above", [B, E, E])
        equal = sb("equal", [B, E, E])
        before = sb("before", [B, E, E])
        rank = sb("rank", [B, E])
        picked = sb("picked", [B, BR])
        spread = sb("spread", [B, BR, B])

        parts = sb("parts", [P, 8, KC, FILL], F16)
        P_HI, P_LO, A_HI, A_LO, Q_HI, Q_LO, H_HI, H_LO = range(8)
        tanh_out = sb("tanh_out", [P, GATES, ST])
        st = sb("st", [P, 9, ST])
        PP, V, VV, A, AA, ZZ, QQ, HK, HH = range(9)

        gate_ps = [pb("r_ps"), pb("z_ps"), pb("c_ps")]
        up_ps = [pb("up0_ps"), pb("up1_ps")]
        y_ps = pb("y_ps")
        xp_ps = [pb("xp0_ps"), pb("xp1_ps")]
        rows_ps = xp_ps[1]
        gate_v = [g[:, 0:KC * SC].rearrange("p (m s b) -> p m s b", m=KC, b=B) for g in gate_ps]

        x_in = [sem(f"x_in{i}") for i in range(CH)]
        small_in = sem("small_in")
        mats_in = sem("mats_in")
        ident_made = sem("ident_made")
        pool_chain = sem("pool_chain")
        pool_passed = sem("pool_passed")
        act_passed = sem("act_passed")
        x_turned = sem("x_turned")
        x_copied = sem("x_copied")
        rows_turned = sem("rows_turned")
        cols_copied = sem("cols_copied")
        umax_local = sem("umax_local")
        umax_shared = sem("umax_shared")
        setup_chain = sem("setup_chain")
        gbias_summed = sem("gbias_summed")
        silu_tanh = sem("silu_tanh")
        silu_made = sem("silu_made")
        agg_made = sem("agg_made")
        logits_made = sem("logits_made")
        logits_shifted = sem("logits_shifted")
        exp_made = sem("exp_made")
        spread_made = sem("spread_made")
        weights_shared = sem("weights_shared")
        scales_made = sem("scales_made")
        up_in = [sem(f"up_in{e}") for e in range(BR)]
        down_in = [sem(f"down_in{e}") for e in range(BR)]
        up_done = sem("up_done")
        down_done = sem("down_done")
        gelu_done = sem("gelu_done")
        scaled = sem("scaled")
        bias1_ready = sem("bias1_ready")
        feat_ready = sem("feat_ready")
        xp_done = sem("xp_done")
        xp_ready = sem("xp_ready")
        split_ready = sem("split_ready")
        injected = sem("injected")
        preact = sem("preact")
        act_done = sem("act_done")
        part_ready = sem("part_ready")
        state = sem("state")
        body_h = sem("body_h")
        body_added = sem("body_added")
        h_unscaled = sem("h_unscaled")
        turned = sem("turned")
        turned_copied = sem("turned_copied")
        out_written = sem("out_written")

        PARTS_STEP, STATE_STEP = 8, 9
        block = ctx.enter_context(nc.Block())

        def scale_tile(engine, c, e, half=None):
            at, width = (0, COLS) if half is None else (half * HALF, HALF)
            cols = hidden[:, e % 2, at:at + width]
            if e in (1, 2):
                w = gate_scale[:, e - 1, bass.ds(c * COLS + at, width)]
            else:
                cols = cols.rearrange("p (t b) -> p t b", b=B)
                w = expert_w[:, e, :].unsqueeze(1).broadcast_to([P, width // B, B])
            engine.tensor_tensor(cols, cols, w, ALU.mult).then_inc(scaled, 2 if half is None else 1)

        @block.sync
        def _(sp):
            for i in range(CH):
                sp.dma_start(x_rows[:, i, :, :],
                             x[:, i * P:(i + 1) * P, :].rearrange("b p d -> p b d")).then_inc(x_in[i], 16)
            sp.sem_inc(up_done, BR)
            sp.sem_inc(down_done, BR)
            sp.sem_inc(out_written, 2 * 16)

            def load_tile(c, j):
                units = c * (BODIES * BR) + j * BR
                for e in range(BR):
                    w1 = ew1[e, :, :] if e < E else sw1
                    w2 = ew2[e, :, :] if e < E else sw2
                    sp.wait_ge(up_done, units + (e + 1))
                    sp.dma_start(up_w[:, e, :, :],
                                 w1.rearrange("(k p) n -> p k n", p=P)[:, :, bass.ds(j * P, P)]
                                 ).then_inc(up_in[e], 16)
                    sp.wait_ge(down_done, units + (e + 1))
                    sp.dma_start(down_w[:, e, :], w2[bass.ds(j * P, P), :]).then_inc(down_in[e], 16)

            def store_body(n):
                sp.wait_ge(turned_copied, n + 2)
                for b in range(B):
                    sp.dma_start(out[b, bass.ds(n * STEPS, STEPS), :], out_rows[b:SC:B, :]
                                 ).then_inc(out_written, 16)

            lag = LEAD + 2
            with sp.Fori(0, lag // BODIES) as c:
                with sp.Fori(0, BODIES) as j:
                    load_tile(c, j)
            with sp.Fori(0, lag % BODIES) as j:
                load_tile(lag // BODIES, j)
            with sp.Fori(lag % BODIES, BODIES) as j:
                load_tile(lag // BODIES, j)
                store_body(j + (lag // BODIES * BODIES - lag))
            with sp.Fori(lag // BODIES + 1, CH) as c:
                with sp.Fori(0, BODIES) as j:
                    load_tile(c, j)
                    store_body(c * BODIES + j - lag)
            with sp.Fori(CH * BODIES - lag, CH * BODIES) as n:
                store_body(n)
            sp.wait_ge(out_written, (CH * BODIES + 1) * 2 * 16)

        @block.gpsimd
        def _(pool):
            pool.memset(ones[:, :], 1.0).then_inc(ident_made, 1)
            pool.memset(ident[:, :], 0.0).then_inc(pool_chain, 1)
            pool.wait_ge(pool_chain, 1)
            pool.affine_select(out=ident[:, :], in_=ident[:, :], compare_op=ALU.not_equal, fill=1.0,
                               base=0, pattern=[[-1, P]], channel_multiplier=1).then_inc(ident_made, 1)
            pool.wait_ge(ident_made, 2)
            pool.tensor_copy(ident16[:, :], ident[:, :]).then_inc(ident_made, 1)
            pool.wait_ge(umax_local, 1)
            pool.partition_all_reduce(uall[:, :], umax[:, :], P,
                                      bass.bass_isa.ReduceOp.max).then_inc(umax_shared, 1)
            pool.sem_inc(split_ready, 1)
            pool.memset(out_feat[:, :, :], 0.0).then_inc(body_added, 1)
            CHAIN0, PER_SPLIT = 1, 3

            def wait_apart(semaphore, value):
                pool.wait_ge(semaphore, value)
                pool.sem_inc(pool_passed, 1)

            def split(c, j):
                n = c * BODIES + j
                chain = n * PER_SPLIT + CHAIN0
                src = xpart[:, :, bass.ds(j * SC, SC)]
                if isinstance(j, int) and j == 0:
                    pool.wait_ge(xp_ready, (c + 1) * (GATES * KC * B) + 1)
                wait_apart(injected, n + 1)
                pool.tensor_copy(xsplit[:, 0, :, :], src).then_inc(pool_chain, 1)
                wait_apart(pool_chain, chain + 1)
                pool.tensor_tensor(xrest[:, :, :], src, xsplit[:, 0, :, :],
                                   ALU.subtract).then_inc(pool_chain, 1)
                wait_apart(pool_chain, chain + 2)
                pool.tensor_copy(xsplit[:, 1, :, :], xrest[:, :, :]).then_inc(pool_chain, 1)
                pool.wait_ge(pool_chain, chain + 3)
                pool.tensor_tensor(xsplit[:, 2, :, :], xrest[:, :, :], xsplit[:, 1, :, :],
                                   ALU.subtract).then_inc(split_ready, 1)

            def add_body(c, j):
                n = c * BODIES + j
                wait_apart(body_h, n + 1)
                pool.tensor_scalar(h_true[:, :, :], h_body[:, :, :], w_scale[:, :], None, ALU.mult
                                   ).then_inc(h_unscaled, 1)
                wait_apart(h_unscaled, n + 2)
                wait_apart(turned, n + 1)
                pool.tensor_tensor(out_feat[:, :, :], h_true[:, :, :],
                                   feat[:, :, bass.ds(c * COLS + j * SC, SC)], ALU.add
                                   ).then_inc(body_added, 1)

            def scale_tiles(c, j):
                for e in range(E):
                    wait_apart(gelu_done, (c * BODIES + j) * (2 * BR) + (2 * e + 3))
                    scale_tile(pool, c, e)

            pool.wait_ge(scales_made, 1)
            split(0, 0)
            with pool.Fori(0, CH - 2) as c:
                with pool.Fori(0, BODIES - 1) as j:
                    split(c, j + 1)
                    scale_tiles(c + 1, j + 1)
                    add_body(c, j)
                scale_tiles(c + 2, 0)
                split(c + 1, 0)
                add_body(c, BODIES - 1)
            with pool.Fori(0, BODIES - 1) as j:
                split(CH - 2, j + 1)
                scale_tiles(CH - 1, j + 1)
                add_body(CH - 2, j)
            split(CH - 1, 0)
            add_body(CH - 2, BODIES - 1)
            with pool.Fori(0, BODIES - 1) as j:
                split(CH - 1, j + 1)
                add_body(CH - 1, j)
            add_body(CH - 1, BODIES - 1)

        @block.scalar
        def _(act):
            b1_rows = eb1.rearrange("e (t p) -> e t p", p=P)
            small_count = 0
            for e in range(BR):
                src = b1_rows[e, :, :] if e < E else sb1.rearrange("(t p) -> t p", p=P)
                act.dma_start(small_rows[ROW_B1 + e * HT:ROW_B1 + (e + 1) * HT, :], src).then_inc(small_in, 16)
            for g in range(GATES):
                act.dma_start(small_rows[ROW_BG + g * KC:ROW_BG + (g + 1) * KC, :],
                              b_in[g].rearrange("(k p) -> k p", p=P)).then_inc(small_in, 16)
            act.dma_start(small_rows[ROW_COND:ROW_COND + B * KC, :],
                          cond.rearrange("b (k p) -> (b k) p", p=P)).then_inc(small_in, 16)
            for g in range(GATES):
                act.dma_start(uf[:, g, :, :], u_in[g].rearrange("(k p) n -> p k n", p=P)).then_inc(mats_in, 16)
                act.dma_start(wx[:, g, :, :], w_in[g].rearrange("(k p) n -> p k n", p=P)).then_inc(mats_in, 16)
                act.dma_start(cf[:, g, :, :], c_in[g].rearrange("(k p) n -> p k n", p=P)).then_inc(mats_in, 16)
            act.dma_start(gate_w_sb[:, :, :, :], gate_w.rearrange("(s k p) n -> p s k n", p=P, k=KC)).then_inc(mats_in, 16)
            act.dma_start(time_w_sb[:, :, :], time_w.rearrange("(k p) n -> p k n", p=P)).then_inc(mats_in, 16)
            act.dma_start(bias_row[:, 0:2 * E], time_b.rearrange("(a n) -> a n", a=1)).then_inc(mats_in, 16)
            act.dma_start(bias_row[:, 2 * E:3 * E], gate_b.rearrange("(a n) -> a n", a=1)).then_inc(mats_in, 16)
            act.dma_start(bias2_rows[0:E, :], eb2).then_inc(mats_in, 16)
            act.dma_start(bias2_rows[E:BR, :], sb2.rearrange("(a n) -> a n", a=1)).then_inc(mats_in, 16)
            act.dma_start(mask_rows[:, :], branch_mask).then_inc(mats_in, 16)

            act.sem_inc(gelu_done, 1)
            act.sem_inc(xp_ready, 1)

            act.wait_ge(cols_copied, 1)
            act.activation(cond_tanh[:, :], small_cols[:, ROW_COND:ROW_COND + B * KC], ACT.Tanh,
                           scale=0.5).then_inc(silu_tanh, 1)
            act.wait_ge(logits_shifted, 1)
            act.activation(score[:, :], logit[:, :], ACT.Exp).then_inc(exp_made, 1)

            def bias1(c, j):
                act.wait_ge(gelu_done, (c * BODIES + j) * (2 * BR) + 1)
                act.sem_inc(act_passed, 1)
                src = small_cols[:, 0:BR * HT].rearrange("p (e t) -> p e t", e=BR)
                act.activation(bias1_now[:, :].unsqueeze(2), src[:, :, bass.ds(j, 1)], ACT.Copy
                               ).then_inc(bias1_ready, 1)

            def gelu_ready(c, j, e):
                units = (c * BODIES + j) * BR
                if e == 0:
                    act.wait_ge(bias1_ready, c * BODIES + j + 1)
                act.wait_ge(up_done, units + (BR + e + 1))
                if e != 1:
                    act.wait_ge(down_done, units + (BR if e == 0 else BR + e - 1))

            def gelu(e, half=None):
                cols = slice(0, COLS) if half is None else slice(half * HALF, (half + 1) * HALF)
                act.activation(hidden[:, e % 2, cols], up_ps[e % 2][:, cols], ACT.Gelu_apprx_tanh,
                               bias=bias1_now[:, e:e + 1]).then_inc(gelu_done, 2 if half is None else 1)

            def gate_tanh(t, g):
                act.wait_ge(preact, t * GATES + g + 1)
                act.activation(tanh_out[:, g, :].rearrange("p (m b) -> p m b", b=B),
                               gate_v[g][:, :, t, :], ACT.Tanh,
                               scale=1.0 if g == C else 0.5).then_inc(act_done, 1)

            def input_part(c, g, m, b):
                if m == 0 and b == 0:
                    act.wait_ge(xp_done, c * GATES + (g + 1))
                    if g == 0:
                        act.wait_ge(split_ready, c * BODIES + 1)
                act.activation(
                    xpart[:, g * KC + m, :].rearrange("p (t b) -> p t b", b=B)[:, :, b],
                    xp_ps[g % 2][:, m * COLS:(m + 1) * COLS].rearrange("p (t b) -> p t b", b=B)[:, :, b],
                    ACT.Identity, bias=gate_bias[:, g, m, b:b + 1]).then_inc(xp_ready, 1)

            def copy_rows(n):
                act.wait_ge(out_written, n * (2 * 16))
                act.wait_ge(turned, n + 1)
                act.activation(out_rows[:, :], rows_ps[0:SC, 0:D], ACT.Copy).then_inc(turned_copied, 1)

            def gru_body(c, j, ffn=None, tail=None):
                for t in range(STEPS):
                    for g in range(GATES):
                        gate_tanh(t, g)
                    if ffn and t == 0:
                        bias1(*ffn)
                    if ffn and t in GELU_STEPS:
                        gelu_ready(*ffn, GELU_STEPS[t])
                        gelu(GELU_STEPS[t])
                    if t == 5:
                        copy_rows(c * BODIES + j)
                    if tail is not None:
                        for piece in TAIL_PIECES.get(t, ()):
                            input_part(tail, *piece)
                act.drain()
                act.sem_inc(preact, -STEPS * GATES)

            def feed_forward(c, j):
                bias1(c, j)
                for e in range(BR):
                    gelu_ready(c, j, e)
                    for half in range(2):
                        gelu(e, half)

            with act.Fori(0, BODIES) as j:
                feed_forward(0, j)
            for pieces in TAIL_PIECES.values():
                for piece in pieces:
                    input_part(0, *piece)
            feed_forward(1, 0)
            with act.Fori(0, CH - 2) as c:
                with act.Fori(0, BODIES - 1) as j:
                    gru_body(c, j, ffn=(c + 1, j + 1))
                gru_body(c, BODIES - 1, ffn=(c + 2, 0), tail=c + 1)
            with act.Fori(0, BODIES - 1) as j:
                gru_body(CH - 2, j, ffn=(CH - 1, j + 1))
            gru_body(CH - 2, BODIES - 1, tail=CH - 1)
            with act.Fori(0, BODIES) as j:
                gru_body(CH - 1, j)
            copy_rows(CH * BODIES)

        @block.vector
        def _(dve):
            chain = [0]

            def link(ins):
                chain[0] += 1
                ins.then_inc(setup_chain, 1)
                dve.wait_ge(setup_chain, chain[0])

            dve.memset(before[:, :, :], 0.0)
            dve.memset(parts[:, :, :, :], 0.0).then_inc(part_ready, PARTS_STEP)
            dve.memset(h_body[:, :, :], 0.0)
            dve.sem_inc(h_unscaled, 1)
            link(dve.memset(picked[:, :], 1.0))
            dve.memset(st[:, :, :], 0.0).then_inc(state, STATE_STEP)
            for e in range(1, E):
                dve.memset(before[:, e, 0:e], 1.0)
            link(dve.memset(gate_scale[:, :, :], 0.0))

            dve.wait_ge(rows_turned, 1)
            dve.tensor_copy(small_cols[:, :], y_ps[:, 0:ROWS]).then_inc(cols_copied, 1)

            for i in range(CH):
                dve.wait_ge(x_turned, i + 1)
                dve.tensor_copy(feat[:, :, i * COLS:(i + 1) * COLS].rearrange("p k (t b) -> p k b t", b=B),
                                xp_ps[i % 2][:, :].rearrange("p (k b t) -> p k b t", k=KC, b=B)
                                ).then_inc(x_copied, 1)
            dve.wait_ge(x_copied, CH)

            dve.wait_ge(mats_in, 16 * 16)
            link(dve.tensor_reduce(umax[:, :], uf[:, :, :, :].rearrange("p g k n -> p (g k n)"), AX.X,
                                   ALU.max, apply_absolute_value=True))
            dve.tensor_scalar(umax[:, :], umax[:, :], 2.0 ** -100, None, ALU.max).then_inc(umax_local, 1)
            dve.wait_ge(umax_shared, 1)
            link(dve.tensor_scalar(w_scale[:, :].bitcast(I32), uall[:, :].bitcast(I32), 0x7F800000, None,
                                   ALU.bitwise_and))
            link(dve.reciprocal(w_scale[:, :], w_scale[:, :]))
            link(dve.tensor_scalar(w_scale[:, :], w_scale[:, :], 2.0 ** 14, 2.0 ** 8, ALU.mult, ALU.min))
            link(dve.tensor_scalar(w_scale[:, :], w_scale[:, :], 2.0 ** -15, None, ALU.max))
            link(dve.reciprocal(h_scale[:, :], w_scale[:, :]))
            dve.tensor_scalar(half_s[:, :], h_scale[:, :], 0.5, None, ALU.mult)
            link(dve.tensor_scalar(uf[:, :, :, :], uf[:, :, :, :], w_scale[:, :], FP16_MAX, ALU.mult, ALU.min))
            link(dve.tensor_scalar(uf[:, :, :, :], uf[:, :, :, :], -FP16_MAX, None, ALU.max))
            link(dve.tensor_copy(u_high[:, :, :, :], uf[:, :, :, :]))
            for g in range(GATES):
                dve.tensor_tensor(u_mid[:, g, :, :], uf[:, g, :, :], u_high[:, g, :, :], ALU.subtract)
                last = dve.tensor_scalar(u_low[:, g, :, :], u_high[:, g, :, :],
                                         1.0 / (PLOW if g == C else LOW), None, ALU.mult)
            link(last)

            dve.wait_ge(gbias_summed, 1)
            gb = y_ps[:, 0:GATES * KC * B].rearrange("p (g k b) -> p (g k) b", k=KC, b=B)
            bg = small_cols[:, ROW_BG:ROW_BG + GATES * KC].unsqueeze(2).broadcast_to([P, GATES * KC, B])
            link(dve.tensor_tensor(gate_bias[:, :, :, :].rearrange("p g k b -> p (g k) b"), gb, bg, ALU.add))

            dve.wait_ge(silu_tanh, 1)
            link(dve.scalar_tensor_tensor(cond_silu[:, :], cond_tanh[:, :], 1.0,
                                          small_cols[:, ROW_COND:ROW_COND + B * KC], ALU.add, ALU.mult))
            dve.tensor_scalar(cond_silu[:, :], cond_silu[:, :], 0.5, None, ALU.mult).then_inc(silu_made, 1)

            for s, (lo, hi) in enumerate(((0, THIRD), (THIRD, 2 * THIRD), (2 * THIRD, T))):
                last = dve.tensor_reduce(
                    seg_sum[:, s, :].rearrange("p (k b) -> p k b", b=B),
                    feat[:, :, lo * B:hi * B].rearrange("p k (t b) -> p k b t", b=B), AX.X, ALU.add)
            link(last)
            flat = agg[:, :, :, :].rearrange("p s k b -> p s (k b)")
            dve.tensor_tensor(flat[:, 1, :], seg_sum[:, 0, :], seg_sum[:, 2, :], ALU.add)
            link(dve.tensor_tensor(flat[:, 2, :], seg_sum[:, 1, :], seg_sum[:, 2, :], ALU.add))
            link(dve.tensor_tensor(flat[:, 0, :], flat[:, 1, :], seg_sum[:, 1, :], ALU.add))
            dve.tensor_scalar(flat[:, 0, :], flat[:, 0, :], 1.0 / T, None, ALU.mult)
            dve.tensor_scalar(flat[:, 1:3, :], flat[:, 1:3, :], 1.0 / (T - THIRD), None,
                              ALU.mult).then_inc(agg_made, 1)

            dve.wait_ge(logits_made, 1)
            link(dve.tensor_copy(modul[:, :], y_ps[0:B, 0:2 * E]))
            link(dve.tensor_scalar(modul[:, 0:E], modul[:, 0:E], 1.0, None, ALU.add))
            link(dve.tensor_tensor(logit[:, :], y_ps[0:B, 2 * E:3 * E], modul[:, 0:E], ALU.mult))
            link(dve.tensor_tensor(logit[:, :], logit[:, :], modul[:, E:2 * E], ALU.add))
            link(dve.tensor_reduce(small[:, 0:1], logit[:, :], AX.X, ALU.max))
            dve.tensor_scalar(logit[:, :], logit[:, :], small[:, 0:1], None, ALU.subtract
                              ).then_inc(logits_shifted, 1)
            dve.wait_ge(exp_made, 1)
            link(dve.tensor_reduce(small[:, 1:2], score[:, :], AX.X, ALU.add))
            link(dve.reciprocal(small[:, 2:3], small[:, 1:2]))
            link(dve.tensor_scalar(score[:, :], score[:, :], small[:, 2:3], None, ALU.mult))

            s_j = score[:, :].unsqueeze(1).broadcast_to([B, E, E])
            s_e = score[:, :].unsqueeze(2).broadcast_to([B, E, E])
            dve.tensor_tensor(above[:, :, :], s_j, s_e, ALU.is_gt)
            link(dve.tensor_tensor(equal[:, :, :], s_j, s_e, ALU.is_equal))
            link(dve.tensor_tensor(equal[:, :, :], equal[:, :, :], before[:, :, :], ALU.mult))
            link(dve.tensor_tensor(above[:, :, :], above[:, :, :], equal[:, :, :], ALU.add))
            link(dve.tensor_reduce(rank[:, :], above[:, :, :], AX.X, ALU.add))
            link(dve.scalar_tensor_tensor(picked[:, 0:E], rank[:, :], 1.5, score[:, :], ALU.is_lt, ALU.mult))
            link(dve.tensor_reduce(small[:, 3:4], picked[:, 0:E], AX.X, ALU.add))
            link(dve.tensor_scalar(small[:, 3:4], small[:, 3:4], 1e-8, None, ALU.add))
            link(dve.reciprocal(small[:, 4:5], small[:, 3:4]))
            link(dve.tensor_scalar(picked[:, 0:E], picked[:, 0:E], small[:, 4:5], None, ALU.mult))
            dve.tensor_tensor(spread[:, :, :], picked[:, :].unsqueeze(2).broadcast_to([B, BR, B]),
                              ident[0:B, 0:B].unsqueeze(1).broadcast_to([B, BR, B]), ALU.mult
                              ).then_inc(spread_made, 1)
            dve.wait_ge(weights_shared, 1)
            link(dve.tensor_copy(expert_w[:, :, :].rearrange("p e b -> p (e b)"), y_ps[:, 0:BR * B]))
            wide = gate_scale[:, :, :].rearrange("p e (t b) -> p e t b", b=B)
            for row, e, lo, hi in ((0, 1, 0, THIRD), (0, 1, 2 * THIRD, T), (1, 2, THIRD, T)):
                dve.tensor_copy(wide[:, row, lo:hi, :],
                                expert_w[:, e, :].unsqueeze(1).broadcast_to([P, hi - lo, B]))
            dve.tensor_tensor(branch_rows[:, :].rearrange("e (t b) -> e t b", b=B),
                              mask_rows[:, :].unsqueeze(2).broadcast_to([BR, T, B]),
                              y_ps[0:BR, 16:16 + B].unsqueeze(1).broadcast_to([BR, T, B]), ALU.mult
                              ).then_inc(scales_made, 1)
            dve.wait_ge(scales_made, 1)

            def residual(c, quarter):
                if quarter == 0:
                    dve.wait_ge(down_done, (c + 1) * (BODIES * BR) + BR)
                k, half = divmod(quarter, 2)
                here = feat[:, k, bass.ds(c * COLS + half * HALF, HALF)]
                at = k * COLS + half * HALF
                dve.tensor_tensor(here, y_ps[:, at:at + HALF], here, ALU.add).then_inc(feat_ready, 1)

            def gru_body(c, j, ffn=None, tail=None):
                n = c * BODIES + j
                for t in range(STEPS):
                    gate0 = t * GATES
                    s0 = (t + 1) * STATE_STEP
                    tr, tz, tc = (tanh_out[:, g, :].rearrange("p (m b) -> p m b", b=B) for g in range(GATES))
                    now = h_body[:, :, t * B:(t + 1) * B]
                    prev_t = (t - 1) % STEPS
                    prev = h_body[:, :, prev_t * B:(prev_t + 1) * B]
                    sq = lambda ap: ap.rearrange("p (m b) -> p m b", b=B)
                    s = lambda i: sq(st[:, i, :])
                    p = lambda i: parts[:, i, :, 0:B]

                    dve.wait_ge(act_done, gate0 + 1)
                    dve.wait_ge(state, s0)
                    dve.scalar_tensor_tensor(p(P_HI), tr, 1.0, s(HH), ALU.add, ALU.mult).then_inc(part_ready, 1)
                    dve.scalar_tensor_tensor(s(PP), tr, 1.0, s(HK), ALU.add, ALU.mult).then_inc(state, 1)
                    dve.wait_ge(state, s0 + 1)
                    dve.scalar_tensor_tensor(p(P_LO), p(P_HI), -PLOW, s(PP), ALU.mult, ALU.add
                                             ).then_inc(part_ready, 1)

                    dve.wait_ge(act_done, gate0 + 2)
                    dve.scalar_tensor_tensor(s(VV), tz, 1.0, s(HK), ALU.add, ALU.mult).then_inc(state, 1)
                    dve.scalar_tensor_tensor(s(V), tz, 1.0, s(HH), ALU.add, ALU.mult).then_inc(state, 1)
                    dve.tensor_scalar(s(ZZ), tz, 1.0, half_s[:, :], ALU.add, ALU.mult).then_inc(state, 1)
                    dve.wait_ge(state, s0 + 3)
                    dve.tensor_tensor(p(A_HI), prev, s(V), ALU.subtract).then_inc(part_ready, 1)
                    dve.scalar_tensor_tensor(s(AA), s(VV), -LOW / PLOW, s(HK), ALU.mult, ALU.add
                                             ).then_inc(state, 1)
                    dve.tensor_tensor(s(A), prev, s(V), ALU.subtract).then_inc(state, 1)
                    dve.wait_ge(state, s0 + 5)
                    dve.scalar_tensor_tensor(p(A_LO), p(A_HI), -LOW, s(AA), ALU.mult, ALU.add
                                             ).then_inc(part_ready, 1)

                    dve.wait_ge(act_done, gate0 + 3)
                    dve.tensor_tensor(p(Q_HI), s(ZZ), tc, ALU.mult).then_inc(part_ready, 1)
                    dve.scalar_tensor_tensor(s(QQ), tc, LOW, s(ZZ), ALU.mult, ALU.mult).then_inc(state, 1)
                    dve.wait_ge(state, s0 + 7)
                    dve.scalar_tensor_tensor(p(Q_LO), p(Q_HI), -LOW, s(QQ), ALU.mult, ALU.add
                                             ).then_inc(part_ready, 1)
                    dve.scalar_tensor_tensor(p(H_HI), s(QQ), 1.0 / LOW, s(A), ALU.mult, ALU.add
                                             ).then_inc(part_ready, 1)
                    dve.tensor_tensor(s(HK), s(QQ), s(AA), ALU.add).then_inc(state, 1)
                    def keep_h():
                        return dve.scalar_tensor_tensor(now, s(QQ), 1.0 / LOW, s(A), ALU.mult, ALU.add)
                    if t > 0:
                        last_h = keep_h()
                        if t == STEPS - 1:
                            last_h.then_inc(body_h, 1)
                    dve.wait_ge(state, s0 + 8)
                    dve.scalar_tensor_tensor(p(H_LO), p(H_HI), -LOW, s(HK), ALU.mult, ALU.add
                                             ).then_inc(part_ready, 1)
                    dve.tensor_scalar(s(HH), s(HK), 0.5 / LOW, None, ALU.mult).then_inc(state, 1)
                    if t == 0:
                        dve.wait_ge(h_unscaled, n + 1)
                        keep_h()
                    if tail is not None:
                        for quarter in ((0,), (1,), (2, 3))[t] if t < 3 else ():
                            residual(tail, quarter)
                dve.drain()
                dve.sem_inc(act_done, -STEPS * GATES)
                dve.sem_inc(state, -STEPS * STATE_STEP)

            def feed_forward(c, j):
                for e in range(E):
                    for half in range(2):
                        dve.wait_ge(gelu_done, (c * BODIES + j) * (2 * BR) + (2 * e + half + 2))
                        scale_tile(dve, c, e, half)

            with dve.Fori(0, BODIES) as j:
                feed_forward(0, j)
            for quarter in range(4):
                residual(0, quarter)
            feed_forward(1, 0)
            with dve.Fori(0, CH - 2) as c:
                with dve.Fori(0, BODIES - 1) as j:
                    gru_body(c, j, ffn=(c + 1, j + 1))
                gru_body(c, BODIES - 1, ffn=(c + 2, 0), tail=c + 1)
            with dve.Fori(0, BODIES - 1) as j:
                gru_body(CH - 2, j, ffn=(CH - 1, j + 1))
            gru_body(CH - 2, BODIES - 1, tail=CH - 1)
            with dve.Fori(0, BODIES) as j:
                gru_body(CH - 1, j)

        @block.tensor
        def _(pe):
            mm = pe.matmul

            pe.sem_inc(injected, 1)

            pe.wait_ge(ident_made, 3)
            pe.wait_ge(small_in, 16 * (BR + GATES + 1))
            pe.transpose(y_ps[:, 0:ROWS], small_rows[0:ROWS, :], ident[0:ROWS, 0:ROWS]).then_inc(rows_turned, 1)

            for i in range(CH):
                pe.wait_ge(x_in[i], 16)
                if i >= 2:
                    pe.wait_ge(x_copied, i - 1)
                for k in range(KC):
                    for b in range(B):
                        at = (k * B + b) * P
                        last = pe.transpose(xp_ps[i % 2][:, at:at + P], x_rows[:, i, b, k * P:(k + 1) * P],
                                            ident[:, :])
                last.then_inc(x_turned, 1)

            pe.wait_ge(mats_in, 16 * 16)
            pe.wait_ge(cols_copied, 1)
            cond_v = small_cols[:, ROW_COND:ROW_COND + B * KC].rearrange("p (b k) -> p k b", k=KC)
            for g in range(GATES):
                for m in range(KC):
                    at = (g * KC + m) * B
                    for k in range(KC):
                        last = mm(y_ps[:, at:at + B], cf[:, g, k, m * P:(m + 1) * P], cond_v[:, k, :],
                                  start=(g == 0 and m == 0 and k == 0), stop=(k == KC - 1),
                                  skip_group_check=True)
            last.then_inc(gbias_summed, 1)

            pe.wait_ge(silu_made, 1)
            silu_v = cond_silu[:, :].rearrange("p (b k) -> p k b", k=KC)
            for k in range(KC):
                mm(y_ps[0:B, 0:2 * E], silu_v[:, k, :], time_w_sb[:, k, :], start=(k == 0), stop=False,
                   skip_group_check=True)
            mm(y_ps[0:B, 0:2 * E], ones[0:1, 0:B], bias_row[:, 0:2 * E], start=False, stop=True,
               skip_group_check=True)
            pe.wait_ge(agg_made, 1)
            for s in range(3):
                for k in range(KC):
                    mm(y_ps[0:B, 2 * E:3 * E], agg[:, s, k, :], gate_w_sb[:, s, k, :], start=False, stop=False,
                       skip_group_check=True)
            mm(y_ps[0:B, 2 * E:3 * E], ones[0:1, 0:B], bias_row[:, 2 * E:3 * E], start=False, stop=True,
               skip_group_check=True).then_inc(logits_made, 1)

            pe.wait_ge(spread_made, 1)
            mm(y_ps[:, 0:BR * B], ones[0:B, :], spread[:, :, :].rearrange("q e b -> q (e b)"),
               start=True, stop=True, skip_group_check=True)
            mm(y_ps[0:BR, 16:16 + B], picked[:, :], ident[0:B, 0:B], start=False, stop=True,
               skip_group_check=True).then_inc(weights_shared, 1)

            def output_bias(c):
                for m in range(KC):
                    mm(y_ps[:, m * COLS:(m + 1) * COLS], bias2_rows[:, m * P:(m + 1) * P],
                       branch_rows[:, bass.ds(c * COLS, COLS)],
                       start=(m == 0), stop=False, skip_group_check=True)

            def up_ready(c, j, e):
                n = c * BODIES + j
                pe.wait_ge(up_in[e], (n + 1) * 16)
                if e != 1:
                    pe.wait_ge(gelu_done, n * (2 * BR) + (1 if e == 0 else 2 * e - 1))

            def up(c, e, k, half=None):
                at, width = (0, COLS) if half is None else (half * HALF, HALF)
                last = mm(up_ps[e % 2][:, at:at + width], up_w[:, e, k, :],
                          feat[:, k, bass.ds(c * COLS + at, width)],
                          start=(k == 0 and at == 0), stop=(k == KC - 1), skip_group_check=True)
                if k == KC - 1 and half != 0:
                    last.then_inc(up_done, 1)

            def down_ready(c, j, e):
                n = c * BODIES + j
                pe.wait_ge(down_in[e], (n + 1) * 16)
                if e < E:
                    pe.wait_ge(scaled, n * (2 * E) + (2 * e + 2))
                else:
                    pe.wait_ge(gelu_done, (n + 1) * (2 * BR) + 1)

            def down(e, m, half=None):
                at, width = (0, COLS) if half is None else (half * HALF, HALF)
                last = mm(y_ps[:, m * COLS + at:m * COLS + at + width], down_w[:, e, m * P:(m + 1) * P],
                          hidden[:, e % 2, at:at + width],
                          start=False, stop=(m == KC - 1), skip_group_check=True)
                if m == KC - 1 and half != 0:
                    last.then_inc(down_done, 1)

            def gate_input(c, g, m, k):
                if m == 0 and k == 0:
                    if g == 0:
                        pe.wait_ge(feat_ready, (c + 1) * 4)
                    else:
                        pe.wait_ge(xp_ready, c * (GATES * KC * B) + (g - 1) * (KC * B) + 1)
                last = mm(xp_ps[g % 2][:, m * COLS:(m + 1) * COLS], wx[:, g, k, m * P:(m + 1) * P],
                          feat[:, k, bass.ds(c * COLS, COLS)], start=(m == 0 and k == 0),
                          stop=(k == KC - 1), skip_group_check=True)
                if m == KC - 1 and k == KC - 1:
                    last.then_inc(xp_done, 1)

            def turn_body(n):
                pe.wait_ge(body_added, n + 1)
                for k in range(KC):
                    last = pe.transpose(rows_ps[0:SC, k * P:(k + 1) * P], out_feat[:, k, :], ident[:, :])
                last.then_inc(turned, 1)

            def inject(g, last_of_body):
                for i in range(3):
                    last = mm(gate_ps[g][:, 0:KC * SC], ident16[:, :],
                              xsplit[:, i, g * KC:(g + 1) * KC, :].rearrange("p k n -> p (k n)"),
                              start=(i == 0), stop=(i == 2), skip_group_check=True)
                if last_of_body:
                    last.then_inc(injected, 1)

            def recur(g, t, part, weights, stop=False):
                for m in range(KC):
                    for k in range(KC):
                        for i, w in enumerate(weights):
                            last = mm(gate_ps[g][:, m * SC + t * B:m * SC + t * B + FILL],
                                      w[:, g, k, m * P:(m + 1) * P], parts[:, part, k, :], start=False,
                                      stop=stop and k == KC - 1 and i == len(weights) - 1,
                                      skip_group_check=True)
                return last

            BOTH, DOWNED = (u_high, u_mid), (u_low,)

            def gap_work(c, j, t, window, ffn, tail):
                if t == 1 and window == 1:
                    turn_body(c * BODIES + j)
                if tail is not None and t == 3 and window == 0 and ffn:
                    pe.wait_ge(feat_ready, (tail + 1) * 4)
                    output_bias(tail + 1)
                if ffn:
                    if t == 0 and window == 0:
                        up_ready(*ffn, 0)
                    for kind, e, unit in FFN_UNITS[t, window]:
                        if kind == UP:
                            up(ffn[0], e, unit % 2, unit // 2)
                        else:
                            down(e, unit % 2, unit // 2)
                    for kind, e, unit in FFN_UNITS.get((t + window, 1 - window), ()):
                        if unit == 0:
                            (up_ready if kind == UP else down_ready)(*ffn, e)
                if tail is not None:
                    for product in TAIL_PRODUCTS.get((t, window), ()):
                        gate_input(tail, *product)

            def gru_body(c, j, ffn=None, tail=None):
                n = c * BODIES + j
                for t in range(STEPS):
                    before_n = t * PARTS_STEP
                    if t == 0:
                        pe.wait_ge(split_ready, n + 2)
                        inject(R, False)
                    pe.wait_ge(part_ready, before_n + (A_HI + 1))
                    recur(R, t, A_HI, BOTH)
                    pe.wait_ge(part_ready, before_n + (A_LO + 1))
                    recur(R, t, A_LO, DOWNED)
                    pe.wait_ge(part_ready, before_n + (Q_HI + 1))
                    recur(R, t, Q_HI, BOTH)
                    pe.wait_ge(part_ready, before_n + (Q_LO + 1))
                    recur(R, t, Q_LO, DOWNED, stop=True).then_inc(preact, 1)
                    if t == 0:
                        inject(Z, False)
                        inject(C, True)
                    pe.wait_ge(part_ready, before_n + (H_HI + 1))
                    recur(Z, t, H_HI, BOTH)
                    pe.wait_ge(part_ready, before_n + (H_LO + 1))
                    recur(Z, t, H_LO, DOWNED, stop=True).then_inc(preact, 1)
                    gap_work(c, j, t, 0, ffn, tail)
                    pe.wait_ge(part_ready, before_n + (PARTS_STEP + P_HI + 1))
                    recur(C, t, P_HI, BOTH)
                    pe.wait_ge(part_ready, before_n + (PARTS_STEP + P_LO + 1))
                    recur(C, t, P_LO, DOWNED, stop=True).then_inc(preact, 1)
                    gap_work(c, j, t, 1, ffn, tail)
                pe.drain()
                pe.sem_inc(part_ready, -STEPS * PARTS_STEP)

            def feed_forward(c, j):
                for e in range(BR + 1):
                    if e < BR:
                        up_ready(c, j, e)
                        for k in range(KC):
                            up(c, e, k)
                    if e > 0:
                        down_ready(c, j, e - 1)
                        for m in range(KC):
                            down(e - 1, m)

            pe.wait_ge(scales_made, 1)
            output_bias(0)
            with pe.Fori(0, BODIES) as j:
                feed_forward(0, j)
            pe.wait_ge(feat_ready, 4)
            output_bias(1)
            for products in TAIL_PRODUCTS.values():
                for product in products:
                    gate_input(0, *product)
            feed_forward(1, 0)
            with pe.Fori(0, CH - 2) as c:
                with pe.Fori(0, BODIES - 1) as j:
                    gru_body(c, j, ffn=(c + 1, j + 1))
                gru_body(c, BODIES - 1, ffn=(c + 2, 0), tail=c + 1)
            with pe.Fori(0, BODIES - 1) as j:
                gru_body(CH - 2, j, ffn=(CH - 1, j + 1))
            gru_body(CH - 2, BODIES - 1, tail=CH - 1)
            with pe.Fori(0, BODIES) as j:
                gru_body(CH - 1, j)
            turn_body(CH * BODIES)


_INS = ['x', 'cond_1024', 'L0_cond_gate_w', 'L0_cond_gate_b', 'L0_cond_time_w', 'L0_cond_time_b',
        'L0_cond_ew1', 'L0_cond_eb1', 'L0_cond_ew2', 'L0_cond_eb2', 'L0_cond_sw1', 'L0_cond_sb1',
        'L0_cond_sw2', 'L0_cond_sb2', 'L1_cond_W_z', 'L1_cond_U_z', 'L1_cond_C_z', 'L1_cond_b_z',
        'L1_cond_W_r', 'L1_cond_U_r', 'L1_cond_C_r', 'L1_cond_b_r', 'L1_cond_W', 'L1_cond_U',
        'L1_cond_C', 'L1_cond_b']


def kernel(**inputs):
    import concourse.bacc as bacc
    from concourse.bass_utils import run_bass_kernel_spmd

    nc = bacc.Bacc("TRN2", target_bir_lowering=False, num_devices=1)
    arrays = {f"in_{name}": np.ascontiguousarray(inputs[name]) for name in _INS}
    b, t, d = arrays["in_x"].shape
    branches = arrays["in_L0_cond_ew1"].shape[0] + 1
    mask = np.ones((branches, t), np.float32)
    mask[1, t // 3:2 * (t // 3)] = 0.0
    mask[2, :t // 3] = 0.0
    arrays["in_branch_mask"] = mask
    args = [nc.dram_tensor(name, a.shape, mybir.dt.from_np(a.dtype), kind="ExternalInput").ap()
            for name, a in arrays.items()]
    out = nc.dram_tensor("out", (b, t, d), F32, kind="ExternalOutput").ap()
    moe_gru_kernel(nc, *args, out)
    r = run_bass_kernel_spmd(nc, [arrays], core_ids=[0])
    return r.results[0]["out"]
```

```python
from contextlib import ExitStack

import numpy as np

import concourse.bass as bass
from concourse import mybir

ALU = mybir.AluOpType
ACT = mybir.ActivationFunctionType
AX = mybir.AxisListType
F32 = mybir.dt.float32
F16 = mybir.dt.float16
BF16 = mybir.dt.bfloat16
I32 = mybir.dt.int32

P = 128
GATES = 3
R, Z, C = range(GATES)
STEPS = 16
LOW = 1024.0
PLOW = 2048.0
FP16_MAX = 65504.0
ROUND = 2 * STEPS
LEAD = 9
FILL = 40


def moe_gru_kernel(nc, x, cond, gate_w, gate_b, time_w, time_b, ew1, eb1, ew2, eb2, sw1, sb1, sw2, sb2,
                   w_z, u_z, c_z, b_z, w_r, u_r, c_r, b_r, w_h, u_h, c_h, b_h, branch_mask, out):
    B, T, D = x.shape
    E, _, H = ew1.shape
    BR = E + 1
    KC = D // P
    TC = P
    CH = T // TC
    COLS = TC * B
    HALF = COLS // 2
    BODIES = TC // STEPS
    HT = H // P
    SC = STEPS * B
    ST = KC * B
    THIRD = T // 3
    assert HT == BODIES and KC == 2 and B == 2 and D == 2 * P and BODIES % 2 == 0

    w_in = [w_r, w_z, w_h]
    u_in = [u_r, u_z, u_h]
    c_in = [c_r, c_z, c_h]
    b_in = [b_r, b_z, b_h]

    UP, DOWN = "up", "down"
    order = [(UP, 0), (UP, 1)]
    for e in range(2, BR):
        order += [(DOWN, e - 2), (UP, e)]
    order += [(DOWN, BR - 2), (DOWN, BR - 1)]
    units = [(kind, e, unit) for kind, e in order for unit in range(4)]
    FFN_UNITS = {}
    for t in range(STEPS):
        for window in range(2):
            count = 2 if window == 1 and t in (4, 5, 6, 7, 8, 9, 10, 12, 14) else 1
            FFN_UNITS[t, window] = [units.pop(0) for _ in range(min(count, len(units)))]
    assert not units
    GELU_STEPS = {t + window: e for (t, window), some in FFN_UNITS.items()
                  for kind, e, unit in some if kind == UP and unit == 3}
    products = [(g, m, k) for g in range(GATES) for m in range(KC) for k in range(KC)]
    windows = [(4, 1), (5, 0), (5, 1), (6, 0), (6, 1), (7, 0), (7, 1), (8, 0), (9, 1), (10, 0), (10, 1), (11, 0)]
    TAIL_PRODUCTS = {w: (p,) for w, p in zip(windows, products)}
    pieces = [(g, m, b) for g in range(GATES) for m in range(KC) for b in range(B)]
    TAIL_PIECES = {t: [] for t in (6, 7, 8, 9, 10, 11, 12, 13)}
    for t, p in zip((6, 6, 7, 8, 9, 9, 10, 10, 11, 12, 13, 13), pieces):
        TAIL_PIECES[t].append(p)

    ROW_B1, ROW_BG, ROW_COND = 0, BR * HT, BR * HT + GATES * KC
    ROWS = ROW_COND + B * KC

    ctx = ExitStack()
    with ctx:
        def sb(name, shape, dt=F32):
            return ctx.enter_context(nc.sbuf_tensor(name, shape, dt))

        def pb(name):
            return ctx.enter_context(nc.psum_tensor(name, [P, 512], F32))

        def sem(name):
            return ctx.enter_context(nc.semaphore(name))

        x_rows = sb("x_rows", [P, CH, B, D])
        feat = sb("feat", [P, KC, T * B])
        gate_scale = sb("gate_scale", [P, 2, T * B])
        expert_w = sb("expert_w", [P, BR, B])
        branch_rows = sb("branch_rows", [BR, T * B])
        branch_w = sb("branch_w", [BR, B])
        mask_rows = sb("mask_rows", [BR, T])
        bias2_rows = sb("bias2_rows", [BR, D])
        up_w = sb("up_w", [P, BR, KC, P])
        down_w = sb("down_w", [P, BR, D])
        hidden = sb("hidden", [P, 2, COLS])
        bias1_now = sb("bias1_now", [P, BR])
        small_rows = sb("small_rows", [P, P])
        small_cols = sb("small_cols", [P, ROWS])
        wx = sb("wx", [P, GATES, KC, D])
        uf = sb("uf", [P, GATES, KC, D])
        cf = sb("cf", [P, GATES, KC, D])
        u_high = sb("u_high", [P, GATES, KC, D], F16)
        u_mid = sb("u_mid", [P, GATES, KC, D], F16)
        u_low = sb("u_low", [P, GATES, KC, D], F16)
        gate_bias = sb("gate_bias", [P, GATES, KC, B])
        xpart = sb("xpart", [P, GATES * KC, COLS])
        xrest = sb("xrest", [P, GATES * KC, SC])
        xsplit = sb("xsplit", [P, 3, GATES * KC, SC], BF16)
        h_body = sb("h_body", [P, KC, SC])
        h_true = sb("h_true", [P, KC, SC])
        out_feat = sb("out_feat", [P, KC, SC])
        out_rows = sb("out_rows", [SC, D])
        ident = sb("ident", [P, P])
        ident16 = sb("ident16", [P, P], BF16)
        ones = sb("ones", [P, P])
        gate_w_sb = sb("gate_w_sb", [P, 3, KC, E])
        time_w_sb = sb("time_w_sb", [P, KC, 2 * E])
        bias_row = sb("bias_row", [1, 3 * E])
        umax = sb("umax", [P, 1])
        uall = sb("uall", [P, 1])
        w_scale = sb("w_scale", [P, 1])
        h_scale = sb("h_scale", [P, 1])
        half_s = sb("half_s", [P, 1])
        seg_sum = sb("seg_sum", [P, 3, KC * B])
        agg = sb("agg", [P, 3, KC, B])
        cond_tanh = sb("cond_tanh", [P, B * KC])
        cond_silu = sb("cond_silu", [P, B * KC])
        modul = sb("modul", [B, 2 * E])
        logit = sb("logit", [B, E])
        small = sb("small", [B, 8])
        score = sb("score", [B, E])
        above = sb("above", [B, E, E])
        equal = sb("equal", [B, E, E])
        before = sb("before", [B, E, E])
        rank = sb("rank", [B, E])
        picked = sb("picked", [B, BR])
        spread = sb("spread", [B, BR, B])

        parts = sb("parts", [P, 8, KC, FILL], F16)
        P_HI, P_LO, A_HI, A_LO, Q_HI, Q_LO, H_HI, H_LO = range(8)
        tanh_out = sb("tanh_out", [P, GATES, ST])
        st = sb("st", [P, 9, ST])
        PP, V, VV, A, AA, ZZ, QQ, HK, HH = range(9)

        gate_ps = [pb("r_ps"), pb("z_ps"), pb("c_ps")]
        up_ps = [pb("up0_ps"), pb("up1_ps")]
        y_ps = pb("y_ps")
        xp_ps = [pb("xp0_ps"), pb("xp1_ps")]
        rows_ps = xp_ps[1]
        gate_v = [g[:, 0:KC * SC].rearrange("p (m s b) -> p m s b", m=KC, b=B) for g in gate_ps]

        x_in = [sem(f"x_in{i}") for i in range(CH // 2)]
        small_in = sem("small_in")
        gate_in = sem("gate_in")
        mats_in = sem("mats_in")
        cond_mats_in = sem("cond_mats_in")
        u_chain = sem("u_chain")
        u_split = sem("u_split")
        gate_scales_made = sem("gate_scales_made")
        rows_made = sem("rows_made")
        w_scale_made = sem("w_scale_made")
        expert_w_made = sem("expert_w_made")
        gbias_made = sem("gbias_made")
        ident_made = sem("ident_made")
        pool_chain = sem("pool_chain")
        pool_passed = sem("pool_passed")
        act_passed = sem("act_passed")
        x_turned = sem("x_turned")
        x_copied_dve = sem("x_copied_dve")
        x_copied_act = sem("x_copied_act")
        rows_turned = sem("rows_turned")
        cols_copied = sem("cols_copied")
        umax_local = sem("umax_local")
        umax_shared = sem("umax_shared")
        setup_chain = sem("setup_chain")
        gbias_summed = sem("gbias_summed")
        silu_tanh = sem("silu_tanh")
        silu_made = sem("silu_made")
        agg_made = sem("agg_made")
        logits_made = sem("logits_made")
        logits_shifted = sem("logits_shifted")
        exp_made = sem("exp_made")
        spread_made = sem("spread_made")
        weights_shared = sem("weights_shared")
        scales_made = sem("scales_made")
        up_in = [sem(f"up_in{e}") for e in range(BR)]
        down_in = [sem(f"down_in{e}") for e in range(BR)]
        up_done = sem("up_done")
        down_done = sem("down_done")
        gelu_done = sem("gelu_done")
        scaled = sem("scaled")
        bias1_ready = sem("bias1_ready")
        feat_ready = sem("feat_ready")
        xp_done = sem("xp_done")
        xp_ready = sem("xp_ready")
        split_ready = sem("split_ready")
        injected = sem("injected")
        preact = sem("preact")
        act_done = sem("act_done")
        part_ready = sem("part_ready")
        state = sem("state")
        body_h = sem("body_h")
        body_added = sem("body_added")
        h_unscaled = sem("h_unscaled")
        turned = sem("turned")
        turned_copied = sem("turned_copied")
        out_written = sem("out_written")

        PARTS_STEP, STATE_STEP = 8, 9
        block = ctx.enter_context(nc.Block())

        def scale_tile(engine, c, e, half=None):
            at, width = (0, COLS) if half is None else (half * HALF, HALF)
            cols = hidden[:, e % 2, at:at + width]
            if e in (1, 2):
                w = gate_scale[:, e - 1, bass.ds(c * COLS + at, width)]
            else:
                cols = cols.rearrange("p (t b) -> p t b", b=B)
                w = expert_w[:, e, :].unsqueeze(1).broadcast_to([P, width // B, B])
            engine.tensor_tensor(cols, cols, w, ALU.mult).then_inc(scaled, 2 if half is None else 1)

        @block.sync
        def _(sp):
            for i in range(CH // 2):
                for b in range(B):
                    sp.dma_start(x_rows[:, 2 * i:2 * i + 2, b, :],
                                 x[b, 2 * i * P:(2 * i + 2) * P, :].rearrange("(c p) d -> p c d", p=P)
                                 ).then_inc(x_in[i], 16)
            sp.sem_inc(up_done, BR)
            sp.sem_inc(down_done, BR)
            sp.sem_inc(out_written, 2 * 16)

            def load_tile(c, j):
                units = c * (BODIES * BR) + j * BR
                for e in range(BR):
                    w1 = ew1[e, :, :] if e < E else sw1
                    w2 = ew2[e, :, :] if e < E else sw2
                    sp.wait_ge(up_done, units + (e + 1))
                    sp.dma_start(up_w[:, e, :, :],
                                 w1.rearrange("(k p) n -> p k n", p=P)[:, :, bass.ds(j * P, P)]
                                 ).then_inc(up_in[e], 16)
                    sp.wait_ge(down_done, units + (e + 1))
                    sp.dma_start(down_w[:, e, :], w2[bass.ds(j * P, P), :]).then_inc(down_in[e], 16)

            def store_body(n):
                sp.wait_ge(turned_copied, n + 2)
                for b in range(B):
                    sp.dma_start(out[b, bass.ds(n * STEPS, STEPS), :], out_rows[b:SC:B, :]
                                 ).then_inc(out_written, 16)

            lag = LEAD + 2
            for g in range(GATES):
                sp.dma_start(cf[:, g, :, :], c_in[g].rearrange("(k p) n -> p k n", p=P)).then_inc(cond_mats_in, 16)
            load_tile(0, 0)
            for g in range(GATES):
                for to, source in ((uf, u_in[g]), (wx, w_in[g])):
                    sp.dma_start(to[:, g, :, :], source.rearrange("(k p) n -> p k n", p=P)).then_inc(mats_in, 16)
            with sp.Fori(1, BODIES) as j:
                load_tile(0, j)
            assert lag // BODIES == 1
            with sp.Fori(0, lag % BODIES) as j:
                load_tile(lag // BODIES, j)
            with sp.Fori(lag % BODIES, BODIES) as j:
                load_tile(lag // BODIES, j)
                store_body(j + (lag // BODIES * BODIES - lag))
            with sp.Fori(lag // BODIES + 1, CH) as c:
                with sp.Fori(0, BODIES) as j:
                    load_tile(c, j)
                    store_body(c * BODIES + j - lag)
            with sp.Fori(CH * BODIES - lag, CH * BODIES) as n:
                store_body(n)
            sp.wait_ge(out_written, (CH * BODIES + 1) * 2 * 16)

        @block.gpsimd
        def _(pool):
            pool.memset(ones[:, :], 1.0).then_inc(ident_made, 1)
            pool.memset(ident[:, :], 0.0).then_inc(pool_chain, 1)
            pool.wait_ge(pool_chain, 1)
            pool.affine_select(out=ident[:, :], in_=ident[:, :], compare_op=ALU.not_equal, fill=1.0,
                               base=0, pattern=[[-1, P]], channel_multiplier=1).then_inc(ident_made, 1)
            pool.wait_ge(ident_made, 2)
            pool.tensor_copy(ident16[:, :], ident[:, :]).then_inc(ident_made, 1)
            pool.wait_ge(umax_local, 1)
            pool.partition_all_reduce(uall[:, :], umax[:, :], P,
                                      bass.bass_isa.ReduceOp.max).then_inc(umax_shared, 1)
            pool.sem_inc(split_ready, 1)
            pool.memset(out_feat[:, :, :], 0.0).then_inc(body_added, 1)
            CHAIN0, PER_SPLIT = 1, 3

            def wait_apart(semaphore, value):
                pool.wait_ge(semaphore, value)
                pool.sem_inc(pool_passed, 1)

            def split(c, j):
                n = c * BODIES + j
                chain = n * PER_SPLIT + CHAIN0
                src = xpart[:, :, bass.ds(j * SC, SC)]
                if isinstance(j, int) and j == 0:
                    pool.wait_ge(xp_ready, (c + 1) * (GATES * KC * B) + 1)
                wait_apart(injected, n + 1)
                pool.tensor_copy(xsplit[:, 0, :, :], src).then_inc(pool_chain, 1)
                wait_apart(pool_chain, chain + 1)
                pool.tensor_tensor(xrest[:, :, :], src, xsplit[:, 0, :, :],
                                   ALU.subtract).then_inc(pool_chain, 1)
                wait_apart(pool_chain, chain + 2)
                pool.tensor_copy(xsplit[:, 1, :, :], xrest[:, :, :]).then_inc(pool_chain, 1)
                pool.wait_ge(pool_chain, chain + 3)
                pool.tensor_tensor(xsplit[:, 2, :, :], xrest[:, :, :], xsplit[:, 1, :, :],
                                   ALU.subtract).then_inc(split_ready, 1)

            def add_body(c, j):
                n = c * BODIES + j
                wait_apart(body_h, n + 1)
                pool.tensor_scalar(h_true[:, :, :], h_body[:, :, :], w_scale[:, :], None, ALU.mult
                                   ).then_inc(h_unscaled, 1)
                wait_apart(h_unscaled, n + 2)
                wait_apart(turned, n + 1)
                pool.tensor_tensor(out_feat[:, :, :], h_true[:, :, :],
                                   feat[:, :, bass.ds(c * COLS + j * SC, SC)], ALU.add
                                   ).then_inc(body_added, 1)

            def scale_tiles(c, j):
                for e in range(E):
                    wait_apart(gelu_done, (c * BODIES + j) * (2 * BR) + (2 * e + 3))
                    scale_tile(pool, c, e)

            pool.wait_ge(expert_w_made, 1)
            wide = gate_scale[:, :, :].rearrange("p e (t b) -> p e t b", b=B)
            for row, e, lo, hi in ((0, 1, 2 * THIRD, T), (1, 2, THIRD, T)):
                pool.tensor_copy(wide[:, row, lo:hi, :],
                                 expert_w[:, e, :].unsqueeze(1).broadcast_to([P, hi - lo, B])
                                 ).then_inc(gate_scales_made, 1)

            pool.wait_ge(w_scale_made, 1)
            flat = lambda w: w[:, :, :, :].rearrange("p g k n -> p (g k n)")
            pool.tensor_scalar(flat(uf), flat(uf), w_scale[:, :], FP16_MAX, ALU.mult, ALU.min).then_inc(u_chain, 1)
            pool.wait_ge(u_chain, 1)
            pool.tensor_scalar(flat(uf), flat(uf), -FP16_MAX, None, ALU.max).then_inc(u_chain, 1)
            pool.wait_ge(u_chain, 2)
            pool.tensor_copy(flat(u_high), flat(uf)).then_inc(u_chain, 1)
            pool.wait_ge(u_chain, 3)
            pool.tensor_tensor(flat(u_mid), flat(uf), flat(u_high), ALU.subtract).then_inc(u_split, 1)
            for g in range(GATES):
                pool.tensor_scalar(u_low[:, g, :, :], u_high[:, g, :, :],
                                   1.0 / (PLOW if g == C else LOW), None, ALU.mult).then_inc(u_split, 1)

            pool.wait_ge(scales_made, 1)
            pool.wait_ge(gate_scales_made, 2)
            split(0, 0)
            with pool.Fori(0, CH - 2) as c:
                with pool.Fori(0, BODIES - 1) as j:
                    split(c, j + 1)
                    scale_tiles(c + 1, j + 1)
                    add_body(c, j)
                scale_tiles(c + 2, 0)
                split(c + 1, 0)
                add_body(c, BODIES - 1)
            with pool.Fori(0, BODIES - 1) as j:
                split(CH - 2, j + 1)
                scale_tiles(CH - 1, j + 1)
                add_body(CH - 2, j)
            split(CH - 1, 0)
            add_body(CH - 2, BODIES - 1)
            with pool.Fori(0, BODIES - 1) as j:
                split(CH - 1, j + 1)
                add_body(CH - 1, j)
            add_body(CH - 1, BODIES - 1)

        @block.scalar
        def _(act):
            act.dma_start(small_rows[ROW_B1:ROW_B1 + E * HT, :],
                          eb1.rearrange("e (t p) -> (e t) p", p=P)).then_inc(small_in, 16)
            act.dma_start(small_rows[ROW_B1 + E * HT:ROW_B1 + BR * HT, :],
                          sb1.rearrange("(t p) -> t p", p=P)).then_inc(small_in, 16)
            for g in range(GATES):
                act.dma_start(small_rows[ROW_BG + g * KC:ROW_BG + (g + 1) * KC, :],
                              b_in[g].rearrange("(k p) -> k p", p=P)).then_inc(small_in, 16)
            act.dma_start(small_rows[ROW_COND:ROW_COND + B * KC, :],
                          cond.rearrange("b (k p) -> (b k) p", p=P)).then_inc(small_in, 16)
            act.dma_start(gate_w_sb[:, :, :, :], gate_w.rearrange("(s k p) n -> p s k n", p=P, k=KC)).then_inc(gate_in, 16)
            act.dma_start(time_w_sb[:, :, :], time_w.rearrange("(k p) n -> p k n", p=P)).then_inc(gate_in, 16)
            act.dma_start(bias_row[:, 0:2 * E], time_b.rearrange("(a n) -> a n", a=1)).then_inc(gate_in, 16)
            act.dma_start(bias_row[:, 2 * E:3 * E], gate_b.rearrange("(a n) -> a n", a=1)).then_inc(gate_in, 16)
            act.dma_start(bias2_rows[0:E, :], eb2).then_inc(gate_in, 16)
            act.dma_start(bias2_rows[E:BR, :], sb2.rearrange("(a n) -> a n", a=1)).then_inc(gate_in, 16)
            act.dma_start(mask_rows[:, :], branch_mask).then_inc(gate_in, 16)

            act.sem_inc(gelu_done, 1)
            act.sem_inc(xp_ready, 1)

            for i in range(CH // 2, CH):
                act.wait_ge(x_turned, i + 1)
                act.activation(feat[:, :, i * COLS:(i + 1) * COLS].rearrange("p k (t b) -> p k b t", b=B),
                               xp_ps[i % 2][:, :].rearrange("p (k b t) -> p k b t", k=KC, b=B),
                               ACT.Copy).then_inc(x_copied_act, 1)

            act.wait_ge(cols_copied, 1)
            act.activation(cond_tanh[:, :], small_cols[:, ROW_COND:ROW_COND + B * KC], ACT.Tanh,
                           scale=0.5).then_inc(silu_tanh, 1)
            act.wait_ge(logits_shifted, 1)
            act.activation(score[:, :], logit[:, :], ACT.Exp).then_inc(exp_made, 1)

            def bias1(c, j):
                act.wait_ge(gelu_done, (c * BODIES + j) * (2 * BR) + 1)
                act.sem_inc(act_passed, 1)
                src = small_cols[:, 0:BR * HT].rearrange("p (e t) -> p e t", e=BR)
                act.activation(bias1_now[:, :].unsqueeze(2), src[:, :, bass.ds(j, 1)], ACT.Identity
                               ).then_inc(bias1_ready, 1)

            def gelu_ready(c, j, e):
                units = (c * BODIES + j) * BR
                if e == 0:
                    act.wait_ge(bias1_ready, c * BODIES + j + 1)
                act.wait_ge(up_done, units + (BR + e + 1))
                if e != 1:
                    act.wait_ge(down_done, units + (BR if e == 0 else BR + e - 1))

            def gelu(e, half=None):
                cols = slice(0, COLS) if half is None else slice(half * HALF, (half + 1) * HALF)
                act.activation(hidden[:, e % 2, cols], up_ps[e % 2][:, cols], ACT.Gelu_apprx_tanh,
                               bias=bias1_now[:, e:e + 1]).then_inc(gelu_done, 2 if half is None else 1)

            def gate_tanh(t, g, first):
                act.wait_ge(preact, (first + t) * GATES + g + 1)
                act.activation(tanh_out[:, g, :].rearrange("p (m b) -> p m b", b=B),
                               gate_v[g][:, :, t, :], ACT.Tanh,
                               scale=1.0 if g == C else 0.5).then_inc(act_done, 1)

            def input_part(c, g, m, b):
                if m == 0 and b == 0:
                    act.wait_ge(xp_done, c * GATES + (g + 1))
                    if g == 0:
                        act.wait_ge(split_ready, c * BODIES + 1)
                act.activation(
                    xpart[:, g * KC + m, :].rearrange("p (t b) -> p t b", b=B)[:, :, b],
                    xp_ps[g % 2][:, m * COLS:(m + 1) * COLS].rearrange("p (t b) -> p t b", b=B)[:, :, b],
                    ACT.Identity, bias=gate_bias[:, g, m, b:b + 1]).then_inc(xp_ready, 1)

            def copy_rows(n):
                act.wait_ge(out_written, n * (2 * 16))
                act.wait_ge(turned, n + 1)
                act.activation(out_rows[:, :], rows_ps[0:SC, 0:D], ACT.Copy).then_inc(turned_copied, 1)

            def gru_body(c, j, first, ffn=None, tail=None):
                for t in range(STEPS):
                    for g in range(GATES):
                        gate_tanh(t, g, first)
                    if ffn and t == 0:
                        bias1(*ffn)
                    if ffn and t in GELU_STEPS:
                        gelu_ready(*ffn, GELU_STEPS[t])
                        gelu(GELU_STEPS[t])
                    if t == 5:
                        copy_rows(c * BODIES + j)
                    if tail is not None:
                        for piece in TAIL_PIECES.get(t, ()):
                            input_part(tail, *piece)
                if first > 0:
                    act.drain()
                    act.sem_inc(preact, -ROUND * GATES)

            def feed_forward(c, j):
                bias1(c, j)
                for e in range(BR):
                    gelu_ready(c, j, e)
                    for half in range(2):
                        gelu(e, half)

            feed_forward(0, 0)
            with act.Fori(1, BODIES) as j:
                feed_forward(0, j)
            act.wait_ge(gbias_made, 1)
            for pieces in TAIL_PIECES.values():
                for piece in pieces:
                    input_part(0, *piece)
            feed_forward(1, 0)
            with act.Fori(0, CH - 2) as c:
                with act.Fori(0, BODIES - 2, 2) as j:
                    gru_body(c, j, 0, ffn=(c + 1, j + 1))
                    gru_body(c, j + 1, STEPS, ffn=(c + 1, j + 2))
                gru_body(c, BODIES - 2, 0, ffn=(c + 1, BODIES - 1))
                gru_body(c, BODIES - 1, STEPS, ffn=(c + 2, 0), tail=c + 1)
            with act.Fori(0, BODIES - 2, 2) as j:
                gru_body(CH - 2, j, 0, ffn=(CH - 1, j + 1))
                gru_body(CH - 2, j + 1, STEPS, ffn=(CH - 1, j + 2))
            gru_body(CH - 2, BODIES - 2, 0, ffn=(CH - 1, BODIES - 1))
            gru_body(CH - 2, BODIES - 1, STEPS, tail=CH - 1)
            with act.Fori(0, BODIES, 2) as j:
                gru_body(CH - 1, j, 0)
                gru_body(CH - 1, j + 1, STEPS)
            copy_rows(CH * BODIES)

        @block.vector
        def _(dve):
            chain = [0]

            def link(ins):
                chain[0] += 1
                ins.then_inc(setup_chain, 1)
                dve.wait_ge(setup_chain, chain[0])

            dve.memset(before[:, :, :], 0.0)
            dve.memset(parts[:, :, :, :], 0.0).then_inc(part_ready, PARTS_STEP)
            dve.memset(h_body[:, :, :], 0.0)
            dve.sem_inc(h_unscaled, 1)
            link(dve.memset(picked[:, :], 1.0))
            dve.memset(st[:, :, :], 0.0).then_inc(state, STATE_STEP)
            for e in range(1, E):
                dve.memset(before[:, e, 0:e], 1.0)
            link(dve.memset(gate_scale[:, :, :], 0.0))

            def make_rows(lo, hi):
                return dve.tensor_tensor(
                    branch_rows[:, lo * B:hi * B].rearrange("e (t b) -> e t b", b=B),
                    mask_rows[:, lo:hi].unsqueeze(2).broadcast_to([BR, hi - lo, B]),
                    branch_w[:, :].unsqueeze(1).broadcast_to([BR, hi - lo, B]), ALU.mult)

            for i in range(CH // 2):
                dve.wait_ge(x_turned, i + 1)
                dve.tensor_copy(feat[:, :, i * COLS:(i + 1) * COLS].rearrange("p k (t b) -> p k b t", b=B),
                                xp_ps[i % 2][:, :].rearrange("p (k b t) -> p k b t", k=KC, b=B)
                                ).then_inc(x_copied_dve, 1)

            for s, (lo, hi) in enumerate(((0, THIRD), (THIRD, 2 * THIRD), (2 * THIRD, T))):
                if s == 2:
                    dve.wait_ge(rows_turned, 1)
                    dve.tensor_copy(small_cols[:, :], y_ps[:, 0:ROWS]).then_inc(cols_copied, 1)
                if s == 0:
                    dve.wait_ge(x_copied_dve, CH // 2)
                else:
                    dve.wait_ge(x_copied_act, -(-hi // TC) - CH // 2)
                last = dve.tensor_reduce(
                    seg_sum[:, s, :].rearrange("p (k b) -> p k b", b=B),
                    feat[:, :, lo * B:hi * B].rearrange("p k (t b) -> p k b t", b=B), AX.X, ALU.add)
            link(last)
            flat = agg[:, :, :, :].rearrange("p s k b -> p s (k b)")
            dve.tensor_tensor(flat[:, 1, :], seg_sum[:, 0, :], seg_sum[:, 2, :], ALU.add)
            link(dve.tensor_tensor(flat[:, 2, :], seg_sum[:, 1, :], seg_sum[:, 2, :], ALU.add))
            link(dve.tensor_tensor(flat[:, 0, :], flat[:, 1, :], seg_sum[:, 1, :], ALU.add))
            dve.tensor_scalar(flat[:, 0, :], flat[:, 0, :], 1.0 / T, None, ALU.mult)
            dve.tensor_scalar(flat[:, 1:3, :], flat[:, 1:3, :], 1.0 / (T - THIRD), None,
                              ALU.mult).then_inc(agg_made, 1)

            dve.wait_ge(silu_tanh, 1)
            link(dve.scalar_tensor_tensor(cond_silu[:, :], cond_tanh[:, :], 1.0,
                                          small_cols[:, ROW_COND:ROW_COND + B * KC], ALU.add, ALU.mult))
            dve.tensor_scalar(cond_silu[:, :], cond_silu[:, :], 0.5, None, ALU.mult).then_inc(silu_made, 1)

            dve.wait_ge(logits_made, 1)
            link(dve.tensor_copy(modul[:, :], y_ps[0:B, 0:2 * E]))
            link(dve.tensor_scalar(modul[:, 0:E], modul[:, 0:E], 1.0, None, ALU.add))
            link(dve.tensor_tensor(logit[:, :], y_ps[0:B, 2 * E:3 * E], modul[:, 0:E], ALU.mult))
            link(dve.tensor_tensor(logit[:, :], logit[:, :], modul[:, E:2 * E], ALU.add))
            link(dve.tensor_reduce(small[:, 0:1], logit[:, :], AX.X, ALU.max))
            dve.tensor_scalar(logit[:, :], logit[:, :], small[:, 0:1], None, ALU.subtract
                              ).then_inc(logits_shifted, 1)
            dve.wait_ge(exp_made, 1)
            link(dve.tensor_reduce(small[:, 1:2], score[:, :], AX.X, ALU.add))
            link(dve.reciprocal(small[:, 2:3], small[:, 1:2]))
            link(dve.tensor_scalar(score[:, :], score[:, :], small[:, 2:3], None, ALU.mult))

            s_j = score[:, :].unsqueeze(1).broadcast_to([B, E, E])
            s_e = score[:, :].unsqueeze(2).broadcast_to([B, E, E])
            dve.tensor_tensor(above[:, :, :], s_j, s_e, ALU.is_gt)
            link(dve.tensor_tensor(equal[:, :, :], s_j, s_e, ALU.is_equal))
            link(dve.tensor_tensor(equal[:, :, :], equal[:, :, :], before[:, :, :], ALU.mult))
            link(dve.tensor_tensor(above[:, :, :], above[:, :, :], equal[:, :, :], ALU.add))
            link(dve.tensor_reduce(rank[:, :], above[:, :, :], AX.X, ALU.add))
            link(dve.scalar_tensor_tensor(picked[:, 0:E], rank[:, :], 1.5, score[:, :], ALU.is_lt, ALU.mult))
            link(dve.tensor_reduce(small[:, 3:4], picked[:, 0:E], AX.X, ALU.add))
            link(dve.tensor_scalar(small[:, 3:4], small[:, 3:4], 1e-8, None, ALU.add))
            link(dve.reciprocal(small[:, 4:5], small[:, 3:4]))
            link(dve.tensor_scalar(picked[:, 0:E], picked[:, 0:E], small[:, 4:5], None, ALU.mult))
            dve.tensor_tensor(spread[:, :, :], picked[:, :].unsqueeze(2).broadcast_to([B, BR, B]),
                              ident[0:B, 0:B].unsqueeze(1).broadcast_to([B, BR, B]), ALU.mult
                              ).then_inc(spread_made, 1)
            dve.wait_ge(weights_shared, 1)
            dve.tensor_copy(branch_w[:, :], y_ps[0:BR, 16:16 + B])
            dve.tensor_copy(expert_w[:, :, :].rearrange("p e b -> p (e b)"), y_ps[:, 0:BR * B]
                            ).then_inc(expert_w_made, 1)
            dve.wait_ge(expert_w_made, 1)
            dve.wait_ge(gate_in, 16 * 7)
            make_rows(0, TC).then_inc(scales_made, 1)
            wide = gate_scale[:, :, :].rearrange("p e (t b) -> p e t b", b=B)
            link(dve.tensor_copy(wide[:, 0, 0:THIRD, :], expert_w[:, 1, :].unsqueeze(1).broadcast_to([P, THIRD, B])))

            dve.wait_ge(mats_in, 16 * 2 * GATES)
            link(dve.tensor_reduce(umax[:, :], uf[:, :, :, :].rearrange("p g k n -> p (g k n)"), AX.X,
                                   ALU.max, apply_absolute_value=True))
            dve.tensor_scalar(umax[:, :], umax[:, :], 2.0 ** -100, None, ALU.max).then_inc(umax_local, 1)
            dve.wait_ge(umax_shared, 1)
            link(dve.tensor_scalar(w_scale[:, :].bitcast(I32), uall[:, :].bitcast(I32), 0x7F800000, None,
                                   ALU.bitwise_and))
            link(dve.reciprocal(w_scale[:, :], w_scale[:, :]))
            link(dve.tensor_scalar(w_scale[:, :], w_scale[:, :], 2.0 ** 14, 2.0 ** 8, ALU.mult, ALU.min))
            dve.tensor_scalar(w_scale[:, :], w_scale[:, :], 2.0 ** -15, None, ALU.max).then_inc(w_scale_made, 1)
            dve.wait_ge(w_scale_made, 1)
            link(dve.reciprocal(h_scale[:, :], w_scale[:, :]))
            link(dve.tensor_scalar(half_s[:, :], h_scale[:, :], 0.5, None, ALU.mult))

            dve.wait_ge(gbias_summed, 1)
            gb = gate_ps[0][:, 0:GATES * KC * B].rearrange("p (g k b) -> p (g k) b", k=KC, b=B)
            bg = small_cols[:, ROW_BG:ROW_BG + GATES * KC].unsqueeze(2).broadcast_to([P, GATES * KC, B])
            dve.tensor_tensor(gate_bias[:, :, :, :].rearrange("p g k b -> p (g k) b"), gb, bg, ALU.add
                              ).then_inc(gbias_made, 1)

            def residual(c, quarter):
                if quarter == 0:
                    dve.wait_ge(down_done, (c + 1) * (BODIES * BR) + BR)
                k, half = divmod(quarter, 2)
                here = feat[:, k, bass.ds(c * COLS + half * HALF, HALF)]
                at = k * COLS + half * HALF
                dve.tensor_tensor(here, y_ps[:, at:at + HALF], here, ALU.add).then_inc(feat_ready, 1)

            def gru_body(c, j, first, ffn=None, tail=None):
                n = c * BODIES + j
                for t in range(STEPS):
                    gate0 = (first + t) * GATES
                    s0 = (first + t + 1) * STATE_STEP
                    tr, tz, tc = (tanh_out[:, g, :].rearrange("p (m b) -> p m b", b=B) for g in range(GATES))
                    now = h_body[:, :, t * B:(t + 1) * B]
                    prev_t = (t - 1) % STEPS
                    prev = h_body[:, :, prev_t * B:(prev_t + 1) * B]
                    sq = lambda ap: ap.rearrange("p (m b) -> p m b", b=B)
                    s = lambda i: sq(st[:, i, :])
                    p = lambda i: parts[:, i, :, 0:B]

                    dve.wait_ge(act_done, gate0 + 1)
                    dve.wait_ge(state, s0)
                    dve.scalar_tensor_tensor(p(P_HI), tr, 1.0, s(HH), ALU.add, ALU.mult).then_inc(part_ready, 1)
                    dve.scalar_tensor_tensor(s(PP), tr, 1.0, s(HK), ALU.add, ALU.mult).then_inc(state, 1)
                    dve.wait_ge(state, s0 + 1)
                    dve.scalar_tensor_tensor(p(P_LO), p(P_HI), -PLOW, s(PP), ALU.mult, ALU.add
                                             ).then_inc(part_ready, 1)

                    dve.wait_ge(act_done, gate0 + 2)
                    dve.scalar_tensor_tensor(s(VV), tz, 1.0, s(HK), ALU.add, ALU.mult).then_inc(state, 1)
                    dve.scalar_tensor_tensor(s(V), tz, 1.0, s(HH), ALU.add, ALU.mult).then_inc(state, 1)
                    dve.tensor_scalar(s(ZZ), tz, 1.0, half_s[:, :], ALU.add, ALU.mult).then_inc(state, 1)
                    dve.wait_ge(state, s0 + 3)
                    dve.tensor_tensor(p(A_HI), prev, s(V), ALU.subtract).then_inc(part_ready, 1)
                    dve.scalar_tensor_tensor(s(AA), s(VV), -LOW / PLOW, s(HK), ALU.mult, ALU.add
                                             ).then_inc(state, 1)
                    dve.tensor_tensor(s(A), prev, s(V), ALU.subtract).then_inc(state, 1)
                    dve.wait_ge(state, s0 + 5)
                    dve.scalar_tensor_tensor(p(A_LO), p(A_HI), -LOW, s(AA), ALU.mult, ALU.add
                                             ).then_inc(part_ready, 1)

                    dve.wait_ge(act_done, gate0 + 3)
                    dve.tensor_tensor(p(Q_HI), s(ZZ), tc, ALU.mult).then_inc(part_ready, 1)
                    dve.scalar_tensor_tensor(s(QQ), tc, LOW, s(ZZ), ALU.mult, ALU.mult).then_inc(state, 1)
                    dve.wait_ge(state, s0 + 7)
                    dve.scalar_tensor_tensor(p(Q_LO), p(Q_HI), -LOW, s(QQ), ALU.mult, ALU.add
                                             ).then_inc(part_ready, 1)
                    dve.scalar_tensor_tensor(p(H_HI), s(QQ), 1.0 / LOW, s(A), ALU.mult, ALU.add
                                             ).then_inc(part_ready, 1)
                    dve.tensor_tensor(s(HK), s(QQ), s(AA), ALU.add).then_inc(state, 1)
                    def keep_h():
                        return dve.scalar_tensor_tensor(now, s(QQ), 1.0 / LOW, s(A), ALU.mult, ALU.add)
                    if t > 0:
                        last_h = keep_h()
                        if t == STEPS - 1:
                            last_h.then_inc(body_h, 1)
                    dve.wait_ge(state, s0 + 8)
                    dve.scalar_tensor_tensor(p(H_LO), p(H_HI), -LOW, s(HK), ALU.mult, ALU.add
                                             ).then_inc(part_ready, 1)
                    dve.tensor_scalar(s(HH), s(HK), 0.5 / LOW, None, ALU.mult).then_inc(state, 1)
                    if t == 0:
                        dve.wait_ge(h_unscaled, n + 1)
                        keep_h()
                    if tail is not None:
                        for quarter in ((0,), (1,), (2, 3))[t] if t < 3 else ():
                            residual(tail, quarter)
                if first > 0:
                    dve.drain()
                    dve.sem_inc(act_done, -ROUND * GATES)
                    dve.sem_inc(state, -ROUND * STATE_STEP)

            def feed_forward(c, j):
                for e in range(E):
                    for half in range(2):
                        dve.wait_ge(gelu_done, (c * BODIES + j) * (2 * BR) + (2 * e + half + 2))
                        scale_tile(dve, c, e, half)

            with dve.Fori(0, BODIES) as j:
                feed_forward(0, j)
            for quarter in range(4):
                residual(0, quarter)
            make_rows(TC, T).then_inc(rows_made, 1)
            feed_forward(1, 0)
            with dve.Fori(0, CH - 2) as c:
                with dve.Fori(0, BODIES - 2, 2) as j:
                    gru_body(c, j, 0, ffn=(c + 1, j + 1))
                    gru_body(c, j + 1, STEPS, ffn=(c + 1, j + 2))
                gru_body(c, BODIES - 2, 0, ffn=(c + 1, BODIES - 1))
                gru_body(c, BODIES - 1, STEPS, ffn=(c + 2, 0), tail=c + 1)
            with dve.Fori(0, BODIES - 2, 2) as j:
                gru_body(CH - 2, j, 0, ffn=(CH - 1, j + 1))
                gru_body(CH - 2, j + 1, STEPS, ffn=(CH - 1, j + 2))
            gru_body(CH - 2, BODIES - 2, 0, ffn=(CH - 1, BODIES - 1))
            gru_body(CH - 2, BODIES - 1, STEPS, tail=CH - 1)
            with dve.Fori(0, BODIES, 2) as j:
                gru_body(CH - 1, j, 0)
                gru_body(CH - 1, j + 1, STEPS)

        @block.tensor
        def _(pe):
            mm = pe.matmul

            pe.sem_inc(injected, 1)

            pe.wait_ge(ident_made, 3)
            for i in range(CH):
                if i % 2 == 0:
                    pe.wait_ge(x_in[i // 2], B * 16)
                if i >= 2:
                    if i - 2 < CH // 2:
                        pe.wait_ge(x_copied_dve, i - 1)
                    else:
                        pe.wait_ge(x_copied_act, i - 1 - CH // 2)
                for k in range(KC):
                    for b in range(B):
                        at = (k * B + b) * P
                        last = pe.transpose(xp_ps[i % 2][:, at:at + P], x_rows[:, i, b, k * P:(k + 1) * P],
                                            ident[:, :])
                last.then_inc(x_turned, 1)

            pe.wait_ge(small_in, 16 * (2 + GATES + 1))
            pe.transpose(y_ps[:, 0:ROWS], small_rows[0:ROWS, :], ident[0:ROWS, 0:ROWS]).then_inc(rows_turned, 1)

            pe.wait_ge(gate_in, 16 * 7)
            pe.wait_ge(silu_made, 1)
            silu_v = cond_silu[:, :].rearrange("p (b k) -> p k b", k=KC)
            for k in range(KC):
                mm(y_ps[0:B, 0:2 * E], silu_v[:, k, :], time_w_sb[:, k, :], start=(k == 0), stop=False,
                   skip_group_check=True)
            mm(y_ps[0:B, 0:2 * E], ones[0:1, 0:B], bias_row[:, 0:2 * E], start=False, stop=True,
               skip_group_check=True)
            pe.wait_ge(agg_made, 1)
            for s in range(3):
                for k in range(KC):
                    mm(y_ps[0:B, 2 * E:3 * E], agg[:, s, k, :], gate_w_sb[:, s, k, :], start=False, stop=False,
                       skip_group_check=True)
            mm(y_ps[0:B, 2 * E:3 * E], ones[0:1, 0:B], bias_row[:, 2 * E:3 * E], start=False, stop=True,
               skip_group_check=True).then_inc(logits_made, 1)

            pe.wait_ge(cond_mats_in, 16 * GATES)
            pe.wait_ge(cols_copied, 1)
            cond_v = small_cols[:, ROW_COND:ROW_COND + B * KC].rearrange("p (b k) -> p k b", k=KC)
            for g in range(GATES):
                for m in range(KC):
                    at = (g * KC + m) * B
                    for k in range(KC):
                        last = mm(gate_ps[0][:, at:at + B], cf[:, g, k, m * P:(m + 1) * P], cond_v[:, k, :],
                                  start=(g == 0 and m == 0 and k == 0), stop=(k == KC - 1),
                                  skip_group_check=True)
            last.then_inc(gbias_summed, 1)

            pe.wait_ge(spread_made, 1)
            mm(y_ps[:, 0:BR * B], ones[0:B, :], spread[:, :, :].rearrange("q e b -> q (e b)"),
               start=True, stop=True, skip_group_check=True)
            mm(y_ps[0:BR, 16:16 + B], picked[:, :], ident[0:B, 0:B], start=False, stop=True,
               skip_group_check=True).then_inc(weights_shared, 1)

            def output_bias(c):
                for m in range(KC):
                    mm(y_ps[:, m * COLS:(m + 1) * COLS], bias2_rows[:, m * P:(m + 1) * P],
                       branch_rows[:, bass.ds(c * COLS, COLS)],
                       start=(m == 0), stop=False, skip_group_check=True)

            def chunk_columns(c):
                flat = feat[:, :, :].rearrange("p k n -> p (k n)")
                cols = {}
                for k in range(KC):
                    for half in range(2):
                        at = k * (T * B) + half * HALF + c * COLS
                        at = at if isinstance(at, int) else pe.snap(at)
                        cols[k, half] = flat[:, bass.ds(at, HALF)]
                        if half == 0:
                            cols[k, None] = flat[:, bass.ds(at, COLS)]
                return cols

            def up_ready(c, j, e):
                n = c * BODIES + j
                pe.wait_ge(up_in[e], (n + 1) * 16)
                if e != 1:
                    pe.wait_ge(gelu_done, n * (2 * BR) + (1 if e == 0 else 2 * e - 1))

            def up(cols, e, k, half=None):
                at, width = (0, COLS) if half is None else (half * HALF, HALF)
                last = mm(up_ps[e % 2][:, at:at + width], up_w[:, e, k, :],
                          cols[k, half],
                          start=(k == 0 and at == 0), stop=(k == KC - 1), skip_group_check=True)
                if k == KC - 1 and half != 0:
                    last.then_inc(up_done, 1)

            def down_ready(c, j, e):
                n = c * BODIES + j
                pe.wait_ge(down_in[e], (n + 1) * 16)
                if e < E:
                    pe.wait_ge(scaled, n * (2 * E) + (2 * e + 2))
                else:
                    pe.wait_ge(gelu_done, (n + 1) * (2 * BR) + 1)

            def down(e, m, half=None):
                at, width = (0, COLS) if half is None else (half * HALF, HALF)
                last = mm(y_ps[:, m * COLS + at:m * COLS + at + width], down_w[:, e, m * P:(m + 1) * P],
                          hidden[:, e % 2, at:at + width],
                          start=False, stop=(m == KC - 1), skip_group_check=True)
                if m == KC - 1 and half != 0:
                    last.then_inc(down_done, 1)

            def gate_input(c, cols, g, m, k):
                if m == 0 and k == 0:
                    if g == 0:
                        pe.wait_ge(feat_ready, (c + 1) * 4)
                    else:
                        pe.wait_ge(xp_ready, c * (GATES * KC * B) + (g - 1) * (KC * B) + 1)
                last = mm(xp_ps[g % 2][:, m * COLS:(m + 1) * COLS], wx[:, g, k, m * P:(m + 1) * P],
                          cols[k, None], start=(m == 0 and k == 0),
                          stop=(k == KC - 1), skip_group_check=True)
                if m == KC - 1 and k == KC - 1:
                    last.then_inc(xp_done, 1)

            def turn_body(n):
                pe.wait_ge(body_added, n + 1)
                for k in range(KC):
                    last = pe.transpose(rows_ps[0:SC, k * P:(k + 1) * P], out_feat[:, k, :], ident[:, :])
                last.then_inc(turned, 1)

            def inject(g, last_of_body):
                for i in range(3):
                    last = mm(gate_ps[g][:, 0:KC * SC], ident16[:, :],
                              xsplit[:, i, g * KC:(g + 1) * KC, :].rearrange("p k n -> p (k n)"),
                              start=(i == 0), stop=(i == 2), skip_group_check=True)
                if last_of_body:
                    last.then_inc(injected, 1)

            def recur(g, t, part, weights, stop=False):
                for m in range(KC):
                    for k in range(KC):
                        for i, w in enumerate(weights):
                            last = mm(gate_ps[g][:, m * SC + t * B:m * SC + t * B + FILL],
                                      w[:, g, k, m * P:(m + 1) * P], parts[:, part, k, :], start=False,
                                      stop=stop and k == KC - 1 and i == len(weights) - 1,
                                      skip_group_check=True)
                return last

            BOTH, DOWNED = (u_high, u_mid), (u_low,)

            def gap_work(c, j, t, window, cols, ffn, tail, tail_cols):
                if t == 1 and window == 1:
                    turn_body(c * BODIES + j)
                if tail is not None and t == 3 and window == 0 and ffn:
                    pe.wait_ge(feat_ready, (tail + 1) * 4)
                    output_bias(tail + 1)
                if ffn:
                    if t == 0 and window == 0:
                        up_ready(*ffn, 0)
                    for kind, e, unit in FFN_UNITS[t, window]:
                        if kind == UP:
                            up(cols, e, unit % 2, unit // 2)
                        else:
                            down(e, unit % 2, unit // 2)
                    for kind, e, unit in FFN_UNITS.get((t + window, 1 - window), ()):
                        if unit == 0:
                            (up_ready if kind == UP else down_ready)(*ffn, e)
                if tail is not None:
                    for product in TAIL_PRODUCTS.get((t, window), ()):
                        gate_input(tail, tail_cols, *product)

            def old_state(t, count):
                pe.wait_ge(part_ready, count + (A_HI + 1))
                recur(R, t, A_HI, BOTH)
                pe.wait_ge(part_ready, count + (A_LO + 1))
                recur(R, t, A_LO, DOWNED)

            def gru_body(c, j, first, cols, ffn=None, tail=None, tail_cols=None, last=False):
                n = c * BODIES + j
                for t in range(STEPS):
                    before_n = (first + t) * PARTS_STEP
                    pe.wait_ge(part_ready, before_n + (Q_HI + 1))
                    recur(R, t, Q_HI, BOTH)
                    pe.wait_ge(part_ready, before_n + (Q_LO + 1))
                    recur(R, t, Q_LO, DOWNED, stop=True).then_inc(preact, 1)
                    if t == 0:
                        inject(Z, False)
                        inject(C, True)
                    pe.wait_ge(part_ready, before_n + (H_HI + 1))
                    recur(Z, t, H_HI, BOTH)
                    pe.wait_ge(part_ready, before_n + (H_LO + 1))
                    recur(Z, t, H_LO, DOWNED, stop=True).then_inc(preact, 1)
                    gap_work(c, j, t, 0, cols, ffn, tail, tail_cols)
                    pe.wait_ge(part_ready, before_n + (PARTS_STEP + P_HI + 1))
                    recur(C, t, P_HI, BOTH)
                    pe.wait_ge(part_ready, before_n + (PARTS_STEP + P_LO + 1))
                    recur(C, t, P_LO, DOWNED, stop=True).then_inc(preact, 1)
                    gap_work(c, j, t, 1, cols, ffn, tail, tail_cols)
                    if t < STEPS - 1:
                        old_state(t + 1, before_n + PARTS_STEP)
                    elif not last:
                        pe.wait_ge(split_ready, n + 3)
                        inject(R, False)
                        old_state(0, before_n + PARTS_STEP)
                if first > 0 and not last:
                    pe.drain()
                    pe.sem_inc(part_ready, -ROUND * PARTS_STEP)

            def feed_forward(c, j, cols):
                for e in range(BR + 1):
                    if e < BR:
                        up_ready(c, j, e)
                        for k in range(KC):
                            up(cols, e, k)
                    if e > 0:
                        down_ready(c, j, e - 1)
                        for m in range(KC):
                            down(e - 1, m)

            pe.wait_ge(scales_made, 1)
            output_bias(0)
            with pe.Fori(0, BODIES) as j:
                feed_forward(0, j, chunk_columns(0))
            pe.wait_ge(feat_ready, 4)
            pe.wait_ge(mats_in, 16 * 2 * GATES)
            for products in TAIL_PRODUCTS.values():
                for product in products:
                    gate_input(0, chunk_columns(0), *product)
            pe.wait_ge(rows_made, 1)
            output_bias(1)
            feed_forward(1, 0, chunk_columns(1))
            pe.wait_ge(u_split, 1 + GATES)
            pe.wait_ge(gbias_made, 1)
            pe.wait_ge(split_ready, 2)
            inject(R, False)
            old_state(0, 0)
            with pe.Fori(0, CH - 2) as c:
                cols = chunk_columns(c + 1)
                with pe.Fori(0, BODIES - 2, 2) as j:
                    gru_body(c, j, 0, cols, ffn=(c + 1, j + 1))
                    gru_body(c, j + 1, STEPS, cols, ffn=(c + 1, j + 2))
                gru_body(c, BODIES - 2, 0, cols, ffn=(c + 1, BODIES - 1))
                gru_body(c, BODIES - 1, STEPS, chunk_columns(c + 2), ffn=(c + 2, 0), tail=c + 1, tail_cols=cols)
            cols = chunk_columns(CH - 1)
            with pe.Fori(0, BODIES - 2, 2) as j:
                gru_body(CH - 2, j, 0, cols, ffn=(CH - 1, j + 1))
                gru_body(CH - 2, j + 1, STEPS, cols, ffn=(CH - 1, j + 2))
            gru_body(CH - 2, BODIES - 2, 0, cols, ffn=(CH - 1, BODIES - 1))
            gru_body(CH - 2, BODIES - 1, STEPS, None, tail=CH - 1, tail_cols=cols)
            with pe.Fori(0, BODIES - 2, 2) as j:
                gru_body(CH - 1, j, 0, None)
                gru_body(CH - 1, j + 1, STEPS, None)
            gru_body(CH - 1, BODIES - 2, 0, None)
            gru_body(CH - 1, BODIES - 1, STEPS, None, last=True)
            turn_body(CH * BODIES)


_INS = ['x', 'cond_1024', 'L0_cond_gate_w', 'L0_cond_gate_b', 'L0_cond_time_w', 'L0_cond_time_b',
        'L0_cond_ew1', 'L0_cond_eb1', 'L0_cond_ew2', 'L0_cond_eb2', 'L0_cond_sw1', 'L0_cond_sb1',
        'L0_cond_sw2', 'L0_cond_sb2', 'L1_cond_W_z', 'L1_cond_U_z', 'L1_cond_C_z', 'L1_cond_b_z',
        'L1_cond_W_r', 'L1_cond_U_r', 'L1_cond_C_r', 'L1_cond_b_r', 'L1_cond_W', 'L1_cond_U',
        'L1_cond_C', 'L1_cond_b']


def kernel(**inputs):
    import concourse.bacc as bacc
    from concourse.bass_utils import run_bass_kernel_spmd

    nc = bacc.Bacc("TRN2", target_bir_lowering=False, num_devices=1)
    arrays = {f"in_{name}": np.ascontiguousarray(inputs[name]) for name in _INS}
    b, t, d = arrays["in_x"].shape
    branches = arrays["in_L0_cond_ew1"].shape[0] + 1
    mask = np.ones((branches, t), np.float32)
    mask[1, t // 3:2 * (t // 3)] = 0.0
    mask[2, :t // 3] = 0.0
    arrays["in_branch_mask"] = mask
    args = [nc.dram_tensor(name, a.shape, mybir.dt.from_np(a.dtype), kind="ExternalInput").ap()
            for name, a in arrays.items()]
    out = nc.dram_tensor("out", (b, t, d), F32, kind="ExternalOutput").ap()
    moe_gru_kernel(nc, *args, out)
    r = run_bass_kernel_spmd(nc, [arrays], core_ids=[0])
    return r.results[0]["out"]
```
